# Optimizing a Trainium2 kernel written in Bass

```python
import numpy as np
import jax
import jax.numpy as jnp

def _softmax(x, axis=-1):
    return jax.nn.softmax(x, axis=axis)

def _gelu(x):
    return jax.nn.gelu(x, approximate=True)

def _silu(x):
    return jax.nn.silu(x)

def _sigmoid(x):
    return jax.nn.sigmoid(x)

def _layernorm(x, axis=-1, eps=1e-05):
    m = jnp.mean(x, axis=axis, keepdims=True)
    v = jnp.var(x, axis=axis, keepdims=True)
    return (x - m) / jnp.sqrt(v + eps)

def _scatter_add(tgt, idx, src, axis=0):
    return tgt.at[idx].add(src)

def _segment_sum(src, seg, n):
    return jax.ops.segment_sum(src, seg, n)
kernel_name = 'mk_vit_tower_d1_tok_img256_r4_5d82d7'

def setup_inputs(seed: int=0):
    np.random.seed(seed)
    _w = jnp.asarray

    def _rec_inputs():
        import jax
        import jax.numpy as jnp
        _rk = jax.random.key(seed)
        x = -0.000596345 + 1.00056 * jax.random.normal(jax.random.fold_in(_rk, 1), (64, 64, 64, 3), jnp.float32)
        return x
    x = _rec_inputs()

    def _L0_tok_setup():
        import jax, jax.numpy as jnp
        import numpy as np
        M1 = 20
        M2 = 20

        def _spectral_conv(x, w):
            B, Cin, H, W = x.shape
            x_ft = jnp.fft.rfft2(x, norm='ortho')
            out = jnp.einsum('bixy,ioxy->boxy', x_ft[:, :, :M1, :M2], w.astype(x_ft.dtype))
            out_ft = jnp.zeros((B, w.shape[1], H, W // 2 + 1), dtype=x_ft.dtype)
            out_ft = out_ft.at[:, :, :M1, :M2].set(out)
            return jnp.fft.irfft2(out_ft, s=(H, W), norm='ortho')

        def _gelu(x):
            return jax.nn.gelu(x, approximate=False)
        key = jax.random.key(seed)
        ks = jax.random.split(key, 16)
        B, H, W, width = (16, 64, 64, 32)
        scale = 1.0 / (width * width)
        d = {}
        d['coords'] = jax.random.normal(ks[0], (B, H, W, 3), dtype=jnp.float32)
        d['fc0_w'] = jax.random.normal(ks[1], (3, width), dtype=jnp.float32) * 0.1
        d['fc0_b'] = jnp.zeros((width,), dtype=jnp.float32)
        for i in range(4):
            d[f'sw{i}'] = scale * jax.random.normal(ks[2 + i], (width, width, M1, M2), dtype=jnp.float32)
            d[f'cw{i}'] = jax.random.normal(ks[6 + i], (width, width), dtype=jnp.float32) * 0.1
            d[f'cb{i}'] = jnp.zeros((width,), dtype=jnp.float32)
        d['fc1_w'] = jax.random.normal(ks[10], (width, 64), dtype=jnp.float32) * 0.1
        d['fc1_b'] = jnp.zeros((64,), dtype=jnp.float32)
        d['fc2_w'] = jax.random.normal(ks[11], (64, 1), dtype=jnp.float32) * 0.1
        d['fc2_b'] = jnp.zeros((1,), dtype=jnp.float32)
        return d
    _L0_tok_all = _L0_tok_setup()
    _L0_tok_in = {k: v for k, v in _L0_tok_all.items() if k in ('fc0_w', 'fc0_b', 'sw0', 'cw0', 'cb0', 'sw1', 'cw1', 'cb1', 'sw2', 'cw2', 'cb2', 'sw3', 'cw3', 'cb3', 'fc1_w', 'fc1_b', 'fc2_w', 'fc2_b')}
    del _L0_tok_all

    def _L0_attn_setup():
        import jax, jax.numpy as jnp
        import numpy as np
        GAMMA = 0.96875
        SCALE_BASE = 512.0

        def xpos_rope(x, downscale=False):
            B, S, D = x.shape
            half = D // 2
            inv_freq = 1.0 / 10000.0 ** (jnp.arange(0, D, 2, dtype=jnp.float32) / D)
            pos = jnp.arange(S, dtype=jnp.float32)
            ang = pos[:, None] * inv_freq[None, :]
            sin, cos = (jnp.sin(ang), jnp.cos(ang))
            base = (jnp.arange(0, D, 2, dtype=jnp.float32) + 0.4 * D) / (1.4 * D)
            scale = base[None, :] ** (pos[:, None] / SCALE_BASE)
            if downscale:
                scale = 1.0 / scale
            x1 = x[..., 0::2]
            x2 = x[..., 1::2]
            r1 = (x1 * cos - x2 * sin) * scale
            r2 = (x1 * sin + x2 * cos) * scale
            out = jnp.stack([r1, r2], axis=-1).reshape(B, S, D)
            return out

        def get_D(gamma, seq_len):
            n = jnp.arange(seq_len, dtype=jnp.float32)
            diff = n[:, None] - n[None, :]
            mask = diff >= 0
            D = jnp.where(mask, gamma ** jnp.where(mask, diff, 0.0), 0.0)
            return D

        def _reference_tuple_inner(x, W_Q, W_K, W_V):
            S = x.shape[1]
            D = get_D(GAMMA, S)
            Q = xpos_rope(x @ W_Q, downscale=False)
            K = xpos_rope(x @ W_K, downscale=True)
            V = x @ W_V
            ret = jnp.einsum('bnd,bmd->bnm', Q, K) * D[None, :, :]
            out = jnp.einsum('bnm,bmv->bnv', ret, V)
            return (out, ret)
        key = jax.random.key(seed)
        k1, k2, k3, k4 = jax.random.split(key, 4)
        B, S, d_model, d_k, d_v = (8, 1024, 64, 64, 64)
        x = jax.random.normal(k1, (B, S, d_model), dtype=jnp.float32)
        W_Q = jax.random.normal(k2, (d_model, d_k), dtype=jnp.float32) / d_model
        W_K = jax.random.normal(k3, (d_model, d_k), dtype=jnp.float32) / d_model
        W_V = jax.random.normal(k4, (d_model, d_v), dtype=jnp.float32) / d_model
        return {'x': x, 'W_Q': W_Q, 'W_K': W_K, 'W_V': W_V}
    _L0_attn_all = _L0_attn_setup()
    _L0_attn_in = {k: v for k, v in _L0_attn_all.items() if k in ('W_Q', 'W_K', 'W_V')}
    del _L0_attn_all

    def _L0_ffn_setup():
        import jax, jax.numpy as jnp
        import numpy as np
        TOP_K = 6
        LN_EPS = 1e-05
        key = jax.random.key(seed)
        ks = jax.random.split(key, 4)
        B, S, D, E = (2, 64, 64, 64)
        x = jax.random.normal(ks[0], (B, S, D), dtype=jnp.float32)
        gate_w = jax.random.normal(ks[1], (E, D), dtype=jnp.float32) * 0.02
        lattice_weights = jax.random.normal(ks[2], (E, D, D), dtype=jnp.float32) * 0.02
        out_w = jax.random.normal(ks[3], (D, D), dtype=jnp.float32) * 0.02
        out_b = jnp.zeros((D,), dtype=jnp.float32)
        ln_g = jnp.ones((D,), dtype=jnp.float32)
        ln_b = jnp.zeros((D,), dtype=jnp.float32)
        return {'x': x, 'gate_w': gate_w, 'lattice_weights': lattice_weights, 'out_w': out_w, 'out_b': out_b, 'ln_g': ln_g, 'ln_b': ln_b}
    _L0_ffn_all = _L0_ffn_setup()
    _L0_ffn_in = {k: v for k, v in _L0_ffn_all.items() if k in ('gate_w', 'lattice_weights', 'out_w', 'out_b', 'ln_g', 'ln_b')}
    del _L0_ffn_all
    return {'x': x, 'L0_tok_fc0_w': _L0_tok_in['fc0_w'], 'L0_tok_fc0_b': _L0_tok_in['fc0_b'], 'L0_tok_sw0': _L0_tok_in['sw0'], 'L0_tok_cw0': _L0_tok_in['cw0'], 'L0_tok_cb0': _L0_tok_in['cb0'], 'L0_tok_sw1': _L0_tok_in['sw1'], 'L0_tok_cw1': _L0_tok_in['cw1'], 'L0_tok_cb1': _L0_tok_in['cb1'], 'L0_tok_sw2': _L0_tok_in['sw2'], 'L0_tok_cw2': _L0_tok_in['cw2'], 'L0_tok_cb2': _L0_tok_in['cb2'], 'L0_tok_sw3': _L0_tok_in['sw3'], 'L0_tok_cw3': _L0_tok_in['cw3'], 'L0_tok_cb3': _L0_tok_in['cb3'], 'L0_tok_fc1_w': _L0_tok_in['fc1_w'], 'L0_tok_fc1_b': _L0_tok_in['fc1_b'], 'L0_tok_fc2_w': _L0_tok_in['fc2_w'], 'L0_tok_fc2_b': _L0_tok_in['fc2_b'], 'L0_attn_W_Q': _L0_attn_in['W_Q'], 'L0_attn_W_K': _L0_attn_in['W_K'], 'L0_attn_W_V': _L0_attn_in['W_V'], 'L0_ffn_gate_w': _L0_ffn_in['gate_w'], 'L0_ffn_lattice_weights': _L0_ffn_in['lattice_weights'], 'L0_ffn_out_w': _L0_ffn_in['out_w'], 'L0_ffn_out_b': _L0_ffn_in['out_b'], 'L0_ffn_ln_g': _L0_ffn_in['ln_g'], 'L0_ffn_ln_b': _L0_ffn_in['ln_b']}

def reference(x, L0_tok_fc0_w, L0_tok_fc0_b, L0_tok_sw0, L0_tok_cw0, L0_tok_cb0, L0_tok_sw1, L0_tok_cw1, L0_tok_cb1, L0_tok_sw2, L0_tok_cw2, L0_tok_cb2, L0_tok_sw3, L0_tok_cw3, L0_tok_cb3, L0_tok_fc1_w, L0_tok_fc1_b, L0_tok_fc2_w, L0_tok_fc2_b, L0_attn_W_Q, L0_attn_W_K, L0_attn_W_V, L0_ffn_gate_w, L0_ffn_lattice_weights, L0_ffn_out_w, L0_ffn_out_b, L0_ffn_ln_g, L0_ffn_ln_b):
    import jax
    import jax.numpy as jnp

    def _L0_tok_ref(coords, fc0_w, fc0_b, sw0, cw0, cb0, sw1, cw1, cb1, sw2, cw2, cb2, sw3, cw3, cb3, fc1_w, fc1_b, fc2_w, fc2_b):
        import jax, jax.numpy as jnp
        import numpy as np
        M1 = 20
        M2 = 20

        def _spectral_conv(x, w):
            B, Cin, H, W = x.shape
            x_ft = jnp.fft.rfft2(x, norm='ortho')
            out = jnp.einsum('bixy,ioxy->boxy', x_ft[:, :, :M1, :M2], w.astype(x_ft.dtype))
            out_ft = jnp.zeros((B, w.shape[1], H, W // 2 + 1), dtype=x_ft.dtype)
            out_ft = out_ft.at[:, :, :M1, :M2].set(out)
            return jnp.fft.irfft2(out_ft, s=(H, W), norm='ortho')

        def _gelu(x):
            return jax.nn.gelu(x, approximate=False)
        x = coords @ fc0_w + fc0_b
        x = jnp.transpose(x, (0, 3, 1, 2))
        for sw, cw, cb in ((sw0, cw0, cb0), (sw1, cw1, cb1), (sw2, cw2, cb2), (sw3, cw3, cb3)):
            x1 = _spectral_conv(x, sw)
            x2 = jnp.einsum('bchw,oc->bohw', x, cw) + cb[None, :, None, None]
            x = _gelu(x1 + x2)
        x = jnp.transpose(x, (0, 2, 3, 1))
        x = _gelu(x @ fc1_w + fc1_b)
        return (x @ fc2_w + fc2_b)[..., 0]

    def _L0_attn_ref(x, W_Q, W_K, W_V):
        import jax, jax.numpy as jnp
        import numpy as np
        GAMMA = 0.96875
        SCALE_BASE = 512.0

        def xpos_rope(x, downscale=False):
            B, S, D = x.shape
            half = D // 2
            inv_freq = 1.0 / 10000.0 ** (jnp.arange(0, D, 2, dtype=jnp.float32) / D)
            pos = jnp.arange(S, dtype=jnp.float32)
            ang = pos[:, None] * inv_freq[None, :]
            sin, cos = (jnp.sin(ang), jnp.cos(ang))
            base = (jnp.arange(0, D, 2, dtype=jnp.float32) + 0.4 * D) / (1.4 * D)
            scale = base[None, :] ** (pos[:, None] / SCALE_BASE)
            if downscale:
                scale = 1.0 / scale
            x1 = x[..., 0::2]
            x2 = x[..., 1::2]
            r1 = (x1 * cos - x2 * sin) * scale
            r2 = (x1 * sin + x2 * cos) * scale
            out = jnp.stack([r1, r2], axis=-1).reshape(B, S, D)
            return out

        def get_D(gamma, seq_len):
            n = jnp.arange(seq_len, dtype=jnp.float32)
            diff = n[:, None] - n[None, :]
            mask = diff >= 0
            D = jnp.where(mask, gamma ** jnp.where(mask, diff, 0.0), 0.0)
            return D

        def _reference_tuple_inner(x, W_Q, W_K, W_V):
            S = x.shape[1]
            D = get_D(GAMMA, S)
            Q = xpos_rope(x @ W_Q, downscale=False)
            K = xpos_rope(x @ W_K, downscale=True)
            V = x @ W_V
            ret = jnp.einsum('bnd,bmd->bnm', Q, K) * D[None, :, :]
            out = jnp.einsum('bnm,bmv->bnv', ret, V)
            return (out, ret)
        return _reference_tuple_inner(x, W_Q, W_K, W_V)[0]

    def _L0_ffn_ref(x, gate_w, lattice_weights, out_w, out_b, ln_g, ln_b):
        import jax, jax.numpy as jnp
        import numpy as np
        TOP_K = 6
        LN_EPS = 1e-05
        logits = jnp.einsum('bsd,ed->bse', x, gate_w)
        top_logits, indices = jax.lax.top_k(logits, TOP_K)
        scores = jax.nn.softmax(top_logits, axis=-1)
        W_sel = lattice_weights[indices]
        xW = jnp.einsum('bsd,bskde->bske', x, W_sel)
        lattice_out = jnp.einsum('bske,bsk->bse', xW, scores)
        proj = jnp.einsum('bsd,ed->bse', lattice_out, out_w) + out_b
        h = x + proj
        mu = jnp.mean(h, axis=-1, keepdims=True)
        var = jnp.mean(jnp.square(h - mu), axis=-1, keepdims=True)
        return (h - mu) * jax.lax.rsqrt(var + LN_EPS) * ln_g + ln_b
    h = _L0_tok_ref(x, L0_tok_fc0_w, L0_tok_fc0_b, L0_tok_sw0, L0_tok_cw0, L0_tok_cb0, L0_tok_sw1, L0_tok_cw1, L0_tok_cb1, L0_tok_sw2, L0_tok_cw2, L0_tok_cb2, L0_tok_sw3, L0_tok_cw3, L0_tok_cb3, L0_tok_fc1_w, L0_tok_fc1_b, L0_tok_fc2_w, L0_tok_fc2_b)
    h = h + _L0_attn_ref(_layernorm(h, axis=-1), L0_attn_W_Q, L0_attn_W_K, L0_attn_W_V)
    h = h + _L0_ffn_ref(_layernorm(h, axis=-1), L0_ffn_gate_w, L0_ffn_lattice_weights, L0_ffn_out_w, L0_ffn_out_b, L0_ffn_ln_g, L0_ffn_ln_b)
    return h

_drawn_inputs = setup_inputs


def setup_inputs(seed=0):
    import zlib

    import numpy as np

    out = dict(_drawn_inputs(seed))
    spreads = {'L0_tok_fc0_b': (0.0, 0.1),
     'L0_tok_cb0': (0.0, 0.1),
     'L0_tok_cb1': (0.0, 0.1),
     'L0_tok_cb2': (0.0, 0.1),
     'L0_tok_cb3': (0.0, 0.1),
     'L0_tok_fc1_b': (0.0, 0.1),
     'L0_ffn_out_b': (0.0, 0.1),
     'L0_ffn_ln_g': (1.0, 0.2),
     'L0_ffn_ln_b': (0.0, 0.1)}
    factors = {'L0_tok_sw0': 8.0,
     'L0_tok_sw1': 8.0,
     'L0_tok_sw2': 8.0,
     'L0_tok_sw3': 8.0,
     'L0_ffn_gate_w': 8.0,
     'L0_ffn_lattice_weights': 8.0,
     'L0_ffn_out_w': 8.0}
    for name, (base, spread) in spreads.items():
        noise = np.random.default_rng([zlib.crc32(name.encode()), seed]).standard_normal(out[name].shape)
        drawn = base * np.exp(spread * noise) if base else spread * noise
        out[name] = jnp.asarray(drawn.astype(out[name].dtype))
    for name, factor in factors.items():
        out[name] = (out[name] * factor).astype(out[name].dtype)
    return out
```

```python
from contextlib import ExitStack

import numpy as np

import concourse.bass as bass
from concourse import mybir

F32 = mybir.dt.float32
F32R = mybir.dt.float32r
ALU = mybir.AluOpType
ACT = mybir.ActivationFunctionType
AX_X = mybir.AxisListType.X

IMAGES, HH, WW = 64, 64, 64
CH = 32
MODES = 20
LAYERS = 4
QB = 4
GB = 16
QUADS = GB // QB
GROUPS = IMAGES // GB
HALF = HH // 2
PARITY_MODES = MODES // 2
FOLD = 2 * MODES * 2
SPATIAL = HH * WW
PAD_N = 96
PAD_K = 96
KY_BLOCKS = MODES // 4
PIX = 2
HID = 64
SLOT = 1024
SLOTS = 4
TOKENS = IMAGES * HH
TILES = TOKENS // 128
D = 64
EXPERTS = 64
TOP_K = 6
EPS = 1e-5


def dft_constants():
    w = np.arange(WW)
    ky = np.arange(MODES)
    hp = np.arange(HALF)
    norm = 1.0 / np.sqrt(HH * WW)
    phi = 2 * np.pi * np.outer(w, ky) / WW
    fwd_w = np.zeros((2, WW, PAD_N))
    for s in range(2):
        for p in range(2):
            sign = -1.0 if s * p else 1.0
            at = p * MODES * 2
            fwd_w[s, :, at:at + 2 * MODES:2] = sign * norm * np.cos(phi)
            fwd_w[s, :, at + 1:at + 2 * MODES:2] = -sign * norm * np.sin(phi)
    fwd_h = np.zeros((QB, HALF, 2, 2, PAD_N))
    inv_h = np.zeros((PAD_K, 2, 2, QB, HALF))
    for p in range(2):
        for m in range(PARITY_MODES):
            th = 2 * np.pi * (2 * m + p) * hp / HH
            for b in range(QB):
                at = (m * QB + b) * 2
                fwd_h[b, :, 0, p, at] = np.cos(th)
                fwd_h[b, :, 0, p, at + 1] = -np.sin(th)
                fwd_h[b, :, 1, p, at] = np.sin(th)
                fwd_h[b, :, 1, p, at + 1] = np.cos(th)
                inv_h[at, p, 0, b] = np.cos(th)
                inv_h[at + 1, p, 0, b] = -np.sin(th)
                inv_h[at, p, 1, b] = np.sin(th)
                inv_h[at + 1, p, 1, b] = np.cos(th)
    weight = np.where(ky == 0, 1.0, 2.0)[:, None] * norm
    inv_w = np.zeros((PAD_K, 2, WW))
    for p in range(2):
        for s in range(2):
            sign = -1.0 if s * p else 1.0
            at = p * 2 * MODES
            inv_w[at:at + MODES, s] = sign * weight * np.cos(phi.T)
            inv_w[at + MODES:at + 2 * MODES, s] = -sign * weight * np.sin(phi.T)
    f = np.float32
    return (fwd_w.reshape(128, PAD_N).astype(f), fwd_h.reshape(128, -1).astype(f),
            inv_h.reshape(PAD_K, -1).astype(f), inv_w.reshape(PAD_K, -1).astype(f))


def attention_constants():
    f = np.float32
    gamma, scale_base = 0.96875, 512.0
    even = np.arange(0, D, 2, dtype=f)
    inv_freq = (f(1.0) / f(10000.0) ** (even / f(D))).astype(f)
    pos = np.arange(HH, dtype=f)
    ang = pos[:, None] * inv_freq[None, :]
    sin, cos = np.sin(ang), np.cos(ang)
    base = (even + f(0.4 * D)) / f(1.4 * D)
    scale = base[None, :] ** (pos[:, None] / f(scale_base))
    rope = np.zeros((128, 4, D), f)
    for k, sc in enumerate((scale, 1.0 / scale)):
        for image in range(2):
            rows = slice(image * HH, image * HH + HH)
            rope[rows, 2 * k, 0::2] = cos * sc
            rope[rows, 2 * k, 1::2] = cos * sc
            rope[rows, 2 * k + 1, 0::2] = -sin * sc
            rope[rows, 2 * k + 1, 1::2] = sin * sc
    decay = np.zeros((128, 128), f)
    for image in range(2):
        for m in range(HH):
            n = np.arange(m, HH)
            decay[image * HH + m, image * HH + n] = gamma ** (n - m)
    select = np.zeros((2, EXPERTS, EXPERTS // 2, 2, D), f)
    for e in range(EXPERTS):
        select[:, e, e // 2, e % 2, :] = 1.0
    return rope.reshape(128, -1), decay, select.reshape(128, -1)


def layer_steps():
    s = [("turn", 0, i) for i in range(4)]
    for q in range(QUADS):
        for i in range(4):
            s.append(("dft_w", q, i))
            if q + 1 < QUADS:
                s.append(("turn", q + 1, i))
            if i == 0 and q > 0:
                s.append(("dft_h", q - 1, 0))
    s.append(("dft_h", QUADS - 1, 0))
    s += [("mix", 0, i) for i in range(KY_BLOCKS)]
    s += [("modes_turn", q, i) for q in range(2) for i in range(2)]
    s += [("idft_h", q, i) for q in range(2) for i in range(4)]
    s += [("idft_turn", 0, i) for i in range(4)]
    for q in range(QUADS):
        for i in range(4):
            s.append(("out", q, i))
            if q + 1 < QUADS:
                s.append(("idft_turn", q + 1, i))
            if q + 2 < QUADS:
                if i == 0:
                    s += [("modes_turn", q + 2, p) for p in range(2)]
                s += [("idft_h", q + 2, v) for v in ((), (0,), (1,), (2, 3))[i]]
    return s


def mover(stage, q, i):
    if stage in ("out", "fc1"):
        return "act"
    if stage == "turn":
        return "dve" if q == 0 and i % 2 else "act"
    if stage in ("modes_turn", "fc0"):
        return "act" if i % 2 else "dve"
    if stage in ("idft_h", "idft_turn") and q == 0:
        return "act" if i % 2 else "dve"
    if stage in ("x_turn", "qkv", "y_turn", "gate", "s_turn"):
        return "act" if i % 2 else "dve"
    if stage == "qk_turn":
        return "act" if q else "dve"
    return "dve"


class Steps:

    def __init__(self, steps):
        self.steps = steps
        self.index = {s: k for k, s in enumerate(steps)}
        self.by = [mover(*s) for s in steps]
        self.count = len(steps)
        self.moved = {e: sum(b == e for b in self.by) for e in ("dve", "act")}

    def moved_at(self, k):
        return self.by[k], sum(b == self.by[k] for b in self.by[:k + 1])

    def outputs_of(self, stage, q):
        last = {}
        for k, (st, qq, _) in enumerate(self.steps):
            if (st, qq) == (stage, q):
                e, n = self.moved_at(k)
                last[e] = n
        return last.items()


def head_steps():
    s = []
    for pair in range(2 * QUADS + 1):
        for i in range(4):
            if pair < 2 * QUADS:
                s.append(("fc1", pair, i))
            if i == 1 and pair > 0:
                s.append(("fc2", pair - 1, 0))
    return s


LIFT = Steps([("fc0", q, i) for q in range(QUADS) for i in range(4)])
LAYER = Steps(layer_steps())
HEAD = Steps(head_steps())
GROUP_FILLED = LIFT.count + LAYERS * LAYER.count + HEAD.count
GROUP_MOVED = {e: LIFT.moved[e] + LAYERS * LAYER.moved[e] + HEAD.moved[e] for e in ("dve", "act")}


def flat(t):
    names = " ".join("abcd"[:len(t.shape) - 1])
    return t.rearrange(f"p {names} -> p ({names})") if len(t.shape) > 2 else t


def across(t, n):
    return t.rearrange("p (a k) -> p a k", a=1).broadcast_to([t.shape[0], n, t.shape[1]])


def along(t, n):
    return t.rearrange("p (k a) -> p k a", a=1).broadcast_to([t.shape[0], t.shape[1], n])


def tower(nc, slots, ident, ident_in, h_dram, x, fc0_w, fc0_b, sw, cwt, cb, fc1_w, fc1_b, fc2_w, fc2_b,
          k_fwd_w, k_fwd_h, k_inv_h, k_inv_w):
    with ExitStack() as ctx:
        def sb(name, shape, dt=F32):
            return ctx.enter_context(nc.sbuf_tensor(name, shape, dt))

        def sem(name):
            return ctx.enter_context(nc.semaphore(name))

        fwd_w = sb("fwd_w", [128, PAD_N])
        fwd_h = sb("fwd_h", [128, 2, 2, PAD_N])
        inv_h = sb("inv_h", [PAD_K, 2, 2, 128])
        inv_w = sb("inv_w", [PAD_K, 2 * WW])
        lift_w = sb("lift_w", [PAD_K, QUADS, 128])
        lift_b = sb("lift_b", [128, 1])
        conv_all = sb("conv_all", [128, LAYERS, 128])
        conv_w = sb("conv_w", [128, 128])
        conv_b_all = sb("conv_b_all", [128, LAYERS])
        conv_b = sb("conv_b", [128, 1])
        w1 = sb("w1", [128, 2, 128])
        b1 = sb("b1", [128, 1])
        w2 = sb("w2", [128, 32])
        b2 = sb("b2", [128, 1])
        mode_w = sb("mode_w", [128, KY_BLOCKS * MODES, CH])

        xin = sb("xin", [PAD_K, SPATIAL])
        act_c = sb("act_c", [128, QUADS, SPATIAL])
        big = sb("big", [128, 2, SPATIAL])
        mid = sb("mid", [128, 2, FOLD, CH])
        modes_t = sb("modes_t", [PAD_K, 2, 2, MODES * CH])
        modes = sb("modes", [128, KY_BLOCKS, 2, QUADS, PARITY_MODES, 2 * QB])
        rows = sb("rows", [128, 2, SLOT])

        filled = sem("filled")
        moved = {"dve": sem("moved_dve"), "act": sem("moved_act")}
        const_in = sem("const_in")
        zeroed = sem("zeroed")
        x_in = sem("x_in")
        mode_w_in = sem("mode_w_in")
        conv_w_set = sem("conv_w_set")
        mix_started = sem("mix_started")
        h_out = [sem(f"h_out{b}") for b in range(2)]

        plain = [(fwd_w, k_fwd_w), (fwd_h, k_fwd_h), (inv_h, k_inv_h), (inv_w, k_inv_w)]
        blocks = [(lift_w[3 * b:3 * b + 3, b // QB, (b % QB) * CH:(b % QB + 1) * CH], fc0_w)
                  for b in range(GB)]
        blocks += [(conv_all[b * CH:(b + 1) * CH, :, b * CH:(b + 1) * CH],
                    cwt.rearrange("l c o -> c l o")) for b in range(QB)]
        blocks += [(w1[b * CH:(b + 1) * CH, b // 2, (b % 2) * HID:(b % 2 + 1) * HID], fc1_w)
                   for b in range(QB)]
        blocks += [(w2[b * HID:(b + 1) * HID, b:b + 1], fc2_w) for b in range(2)]
        columns = [(lift_b[b * CH:(b + 1) * CH, :], fc0_b.rearrange("(c a) -> c a", a=1))
                   for b in range(QB)]
        columns += [(conv_b_all[b * CH:(b + 1) * CH, :], cb)
                    for b in range(QB)]
        columns += [(b1[b * HID:(b + 1) * HID, :], fc1_b.rearrange("(c a) -> c a", a=1))
                    for b in range(2)]
        columns += [(b2[:, :], fc2_b.rearrange("(a c) -> a c", a=1).broadcast_to([128, 1]))]
        CONSTS = 16 * (len(plain) + len(blocks) + len(columns))

        block = ctx.enter_context(nc.Block())

        @block.sync
        def _(sp):
            for dst, src in plain:
                sp.dma_start(flat(dst[:]), src).then_inc(const_in, 16)
            sp.dma_start(flat(mode_w[:]), sw[LAYERS - 1]).then_inc(mode_w_in, 16)
            sp.wait_ge(zeroed, 1)
            for dst, src in blocks + columns:
                sp.dma_start(dst, src).then_inc(const_in, 16)
            with sp.Fori(0, GROUPS) as g:
                sp.dma_start(xin[0:3 * GB, :], x[g]).then_inc(x_in, 16)
                with sp.Fori(0, LAYERS) as l:
                    start = g * GROUP_FILLED + LIFT.count + l * LAYER.count
                    sp.wait_ge(filled, start + (LAYER.index["mix", 0, KY_BLOCKS - 1] + 1))
                    sp.dma_start(flat(mode_w[:]), sw[l]).then_inc(mode_w_in, 16)
                for pair in range(2 * QUADS):
                    _, n = HEAD.moved_at(HEAD.index["fc2", pair, 0])
                    sp.wait_ge(moved["dve"], g * GROUP_MOVED["dve"] + (
                        LIFT.moved["dve"] + LAYERS * LAYER.moved["dve"] + n))
                    for b in range(2):
                        dst = h_dram.rearrange("(g i) (u t s) -> g i t u s", g=GROUPS, u=2, t=4)[g, 2 * pair + b]
                        src = rows[b:128:32, pair % 2, :].rearrange("t (u s) -> t u s", u=2)
                        sp.dma_start(dst, src).then_inc(h_out[pair % 2], 16)
            for b in range(2):
                sp.wait_ge(h_out[b], 16 * IMAGES // 2)
            sp.wait_ge(mode_w_in, 16 * (1 + GROUPS * LAYERS))

        def slot_of(k):
            return slots[:, k % SLOTS, :]

        def lift_pe(k, q, i):
            for j in range(2):
                mm = nc.tensor.matmul(slot_of(k)[:, j * 512:(j + 1) * 512], lift_w[:, q, :],
                                      xin[:, i * SLOT + j * 512:i * SLOT + (j + 1) * 512],
                                      start=True, stop=True)
            return mm

        def layer_pe(k, stage, q, i):
            s = slot_of(k)
            if stage == "turn":
                for j in range(8):
                    src = act_c[:, q, (8 * i + j) * 128:(8 * i + j + 1) * 128]
                    mm = nc.tensor.transpose(s[:, j * 128:(j + 1) * 128], src, ident[:, :])
            elif stage == "dft_w":
                xw = big[:, q % 2, :].rearrange("p (c m) -> p c m", c=CH)
                for j in range(8):
                    mm = nc.tensor.matmul(s[:, j * 128:j * 128 + PAD_N], xw[:, 8 * i + j, :],
                                          fwd_w[:, :], start=True, stop=True)
            elif stage == "dft_h":
                y = mid[:, q % 2, :, :].rearrange("p (r a) c -> p r (a c)", r=2)
                for p in range(2):
                    for kb in range(KY_BLOCKS):
                        for r in range(2):
                            at = (p * KY_BLOCKS + kb) * 128
                            mm = nc.tensor.matmul(
                                s[:, p * 512 + kb * PAD_N:p * 512 + (kb + 1) * PAD_N],
                                y[:, r, at:at + 128], fwd_h[:, r, p, :],
                                start=(r == 0), stop=(r == 1))
            elif stage == "mix":
                for kx in range(MODES):
                    m, p = kx // 2, kx % 2
                    dst = s[:, p * 512:p * 512 + 320].rearrange("p (q m b) -> p q m b", q=QUADS,
                                                                m=PARITY_MODES)
                    for j in range(4):
                        rows_j = slice(j * CH, (j + 1) * CH)
                        mm = nc.tensor.matmul(dst[rows_j, :, m, :],
                                              mode_w[rows_j, i * MODES + kx, :],
                                              modes[rows_j, i, p, :, m, :], start=True, stop=True)
            elif stage == "modes_turn":
                for kb in range(KY_BLOCKS):
                    mm = nc.tensor.transpose(s[0:80, kb * 128:(kb + 1) * 128],
                                             modes[:, kb, i, q, :, :].rearrange("p m b -> p (m b)"), ident[:, :])
            elif stage == "idft_h":
                p, v = i // 2, i % 2
                for j in range(2):
                    mm = nc.tensor.matmul(s[:, j * 512:j * 512 + 320], inv_h[:, p, v, :],
                                          modes_t[:, q % 2, p, j * 320:(j + 1) * 320],
                                          start=True, stop=True)
            elif stage == "idft_turn":
                for j in range(8):
                    mm = nc.tensor.transpose(s[0:FOLD, j * 128:(j + 1) * 128],
                                             mid[:, q % 2, :, 8 * i + j], ident[:, :])
            elif stage == "out":
                v = big[:, q % 2, :].rearrange("p (h m) -> p h m", h=HALF)
                for j in range(2):
                    h0 = 8 * i + 4 * j
                    nc.tensor.matmul(s[:, j * 512:(j + 1) * 512], conv_w[:, :],
                                     act_c[:, q, h0 * 128:h0 * 128 + 512],
                                     start=True, stop=False, skip_group_check=True)
                    for h in range(4):
                        at = j * 512 + h * 128
                        mm = nc.tensor.matmul(s[:, at:at + 128], v[0:PAD_K, h0 + h, :], inv_w[:, :],
                                              start=False, stop=(h == 3), skip_group_check=True)
            return mm

        def head_pe(k, stage, pair, i):
            s = slot_of(k)
            if stage == "fc1":
                src = act_c[:, pair // 2, :]
                for j in range(2):
                    at = i * SLOT + j * 512
                    mm = nc.tensor.matmul(s[:, j * 512:(j + 1) * 512], w1[:, pair % 2, :],
                                          src[:, at:at + 512], start=True, stop=True)
            else:
                for u in range(2):
                    for t in range(4):
                        at = (u * 4 + t) * 512
                        mm = nc.tensor.matmul(s[32 * t:32 * t + 32, u * 512:(u + 1) * 512], w2[:, :],
                                              big[:, pair % 2, at:at + 512], start=True, stop=True)
            return mm

        READS = {"dft_w": "turn", "dft_h": "dft_w", "modes_turn": "mix", "idft_h": "modes_turn",
                 "idft_turn": "idft_h", "out": "idft_turn", "fc2": "fc1"}

        @block.tensor
        def _(pe):
            pe.wait_ge(const_in, CONSTS)
            pe.wait_ge(ident_in, 16)
            with pe.Fori(0, GROUPS) as g:
                at = {e: g * GROUP_MOVED[e] for e in moved}
                pe.wait_ge(x_in, g * 16 + 16)
                for k, (stage, q, i) in enumerate(LIFT.steps):
                    if k >= SLOTS:
                        e, n = LIFT.moved_at(k - SLOTS)
                        pe.wait_ge(moved[e], at[e] + n)
                    lift_pe(k, q, i).then_inc(filled, 1)
                with pe.Fori(0, LAYERS) as l:
                    at = {e: g * GROUP_MOVED[e] + l * LAYER.moved[e] for e in moved}
                    for e in moved:
                        pe.wait_ge(moved[e], at[e] + LIFT.moved[e])
                    for k, (stage, q, i) in enumerate(LAYER.steps):
                        if k >= SLOTS:
                            e, n = LAYER.moved_at(k - SLOTS)
                            pe.wait_ge(moved[e], at[e] + (LIFT.moved[e] + n))
                        if stage in READS and i == 0:
                            for e, n in LAYER.outputs_of(READS[stage], 0 if stage == "modes_turn" else q):
                                pe.wait_ge(moved[e], at[e] + (LIFT.moved[e] + n))
                        if stage == "mix" and i == 0:
                            for e, n in LAYER.outputs_of("dft_h", QUADS - 1):
                                pe.wait_ge(moved[e], at[e] + (LIFT.moved[e] + n))
                            pe.wait_ge(mode_w_in, g * (16 * LAYERS) + (l * 16 + 16))
                        if (stage, q, i) == ("out", 0, 0):
                            pe.wait_ge(conv_w_set, g * (2 * LAYERS) + (l * 2 + 2))
                        if stage == "mix":
                            pe.sem_inc(mix_started, 1)
                        layer_pe(k, stage, q, i).then_inc(filled, 1)
                base = {e: LIFT.moved[e] + LAYERS * LAYER.moved[e] for e in moved}
                at = {e: g * GROUP_MOVED[e] for e in moved}
                for e in moved:
                    pe.wait_ge(moved[e], at[e] + base[e])
                for k, (stage, pair, i) in enumerate(HEAD.steps):
                    if k >= SLOTS:
                        e, n = HEAD.moved_at(k - SLOTS)
                        pe.wait_ge(moved[e], at[e] + (base[e] + n))
                    if stage == "fc2":
                        for e, n in HEAD.outputs_of("fc1", pair):
                            pe.wait_ge(moved[e], at[e] + (base[e] + n))
                    head_pe(k, stage, pair, i).then_inc(filled, 1)
                for e in moved:
                    pe.wait_ge(moved[e], at[e] + (base[e] + HEAD.moved[e]))

        def plain_move(engine, dst, src):
            if engine == "dve":
                return nc.vector.tensor_copy(dst, src)
            return nc.scalar.copy(dst, src)

        def biased_move(engine, dst, src, bias):
            if engine == "dve":
                return nc.vector.tensor_scalar(dst, src, bias, None, ALU.add)
            return nc.scalar.activation(dst, src, ACT.Identity, bias=bias)

        def move(engine, k, stage, q, i, l=None):
            s = slot_of(k)
            if stage == "fc0":
                dst = act_c[:, q, i * SLOT:(i + 1) * SLOT]
                return biased_move(engine, dst, s, lift_b[:, 0:1])
            if stage == "turn":
                dst = big[:, q % 2, :].rearrange("p (c b h) -> p h b c", c=CH, b=QB)[:, 8 * i:8 * i + 8]
                return plain_move(engine, dst, s.rearrange("p (h b c) -> p h b c", h=8, b=QB))
            if stage == "dft_w":
                dst = mid[:, q % 2, :, 8 * i:8 * i + 8].rearrange("p (r a) c -> p c a r", r=2)
                src = s.rearrange("p (c n) -> p c n", c=8)[:, :, 0:FOLD]
                return plain_move(engine, dst, src.rearrange("p c (a r) -> p c a r", r=2))
            if stage == "dft_h":
                for p in range(2):
                    src = s[:, p * 512:p * 512 + KY_BLOCKS * PAD_N].rearrange("p (k n) -> p k n", n=PAD_N)
                    last = plain_move(engine, modes[:, :, p, q, :, :].rearrange("p k m b -> p k (m b)"),
                                      src[:, :, 0:80])
                return last
            if stage == "mix":
                dst = modes[:, i, :, :, :, :].rearrange("p r q m b -> p r (q m b)")
                return plain_move(engine, dst, s.rearrange("p (r n) -> p r n", r=2)[:, :, 0:320])
            if stage == "modes_turn":
                return plain_move(engine, modes_t[0:80, q % 2, i, :], s[0:80, 0:MODES * CH])
            if stage == "idft_h":
                dst = mid[:, q % 2, i * MODES:(i + 1) * MODES, :].rearrange("p k o -> p (k o)")
                src = s.rearrange("p (j n) -> p j n", j=2)[:, :, 0:320]
                return plain_move(engine, dst.rearrange("p (j n) -> p j n", j=2), src)
            if stage == "idft_turn":
                dst = big[0:FOLD, q % 2, :].rearrange("p (h b o) -> p o b h", h=HALF, b=QB)[:, 8 * i:8 * i + 8]
                return plain_move(engine, dst, s[0:FOLD, :].rearrange("p (o b h) -> p o b h", o=8, b=QB))
            if stage == "out":
                return nc.scalar.activation(act_c[:, q, i * SLOT:(i + 1) * SLOT], s, ACT.Gelu,
                                            bias=conv_b[:, 0:1])
            if stage == "fc1":
                return nc.scalar.activation(big[:, q % 2, i * SLOT:(i + 1) * SLOT], s, ACT.Gelu,
                                            bias=b1[:, 0:1])
            if stage == "fc2":
                return nc.vector.tensor_scalar(rows[:, q % 2, :], s, b2[:, 0:1], None, ALU.add)

        def mover_program(engine, eng):
            eng.wait_ge(const_in, CONSTS)
            with eng.Fori(0, GROUPS) as g:
                for k, (stage, q, i) in enumerate(LIFT.steps):
                    if LIFT.by[k] == engine:
                        eng.wait_ge(filled, g * GROUP_FILLED + (k + 1))
                        move(engine, k, stage, q, i).then_inc(moved[engine], 1)
                with eng.Fori(0, LAYERS) as l:
                    start = g * GROUP_FILLED + l * LAYER.count
                    if engine == "dve":
                        eng.wait_ge(moved["act"], g * GROUP_MOVED["act"] + l * LAYER.moved["act"] + LIFT.moved["act"])
                        eng.wait_ge(filled, start + LIFT.count)
                        nc.vector.tensor_copy(conv_b[:, :], conv_b_all[:, bass.ds(l, 1)]).then_inc(conv_w_set, 1)
                        nc.vector.tensor_copy(conv_w[:, :], conv_all[:, bass.ds(l, 1), :].rearrange(
                            "p a n -> p (a n)")).then_inc(conv_w_set, 1)
                    for k, (stage, q, i) in enumerate(LAYER.steps):
                        if LAYER.by[k] == engine:
                            if (stage, q, i) == ("out", 0, 0):
                                eng.wait_ge(conv_w_set, g * (2 * LAYERS) + (l * 2 + 2))
                            eng.wait_ge(filled, start + (LIFT.count + k + 1))
                            move(engine, k, stage, q, i, l).then_inc(moved[engine], 1)
                start = LIFT.count + LAYERS * LAYER.count
                for k, (stage, q, i) in enumerate(HEAD.steps):
                    if HEAD.by[k] == engine:
                        if stage == "fc2" and q >= 2:
                            eng.wait_ge(h_out[q % 2], g * (8 * GB) + 32 * (q // 2))
                        eng.wait_ge(filled, g * GROUP_FILLED + (start + k + 1))
                        move(engine, k, stage, q, i).then_inc(moved[engine], 1)
                if engine == "dve":
                    for b in range(2):
                        eng.wait_ge(h_out[b], g * (8 * GB) + 8 * GB)

        @block.vector
        def _(dve):
            nc.vector.memset(lift_w[:], 0.0)
            nc.vector.memset(conv_all[:], 0.0)
            nc.vector.memset(w1[:], 0.0)
            nc.vector.memset(w2[:], 0.0)
            nc.vector.memset(modes_t[:], 0.0)
            nc.vector.memset(xin[:], 0.0)
            dve.drain().then_inc(zeroed, 1)
            mover_program("dve", dve)

        @block.scalar
        def _(act):
            mover_program("act", act)


def centre(nc, link, src, centred, squares, stats):
    link(nc.vector.tensor_reduce(stats[:, 0, :], src, AX_X, ALU.add))
    link(nc.vector.tensor_scalar(stats[:, 1, :], stats[:, 0, :], -1.0 / D, None, ALU.mult))
    link(nc.vector.tensor_tensor(centred, src, along(stats[:, 1, :], D), ALU.add))
    link(nc.vector.tensor_tensor(squares, centred, centred, ALU.mult))
    link(nc.vector.tensor_reduce(stats[:, 0, :], squares, AX_X, ALU.add))
    return nc.vector.tensor_scalar(stats[:, 1, :], stats[:, 0, :], 1.0 / D, EPS, ALU.mult, ALU.add)


def root(nc, stats):
    return nc.scalar.activation(stats[:, 2, :], stats[:, 1, :], ACT.Sqrt)


def invert_root(nc, link, stats):
    link(nc.vector.reciprocal(stats[:, 0, :], stats[:, 2, :]))
    link(nc.vector.tensor_tensor(stats[:, 0, :], stats[:, 0, :], stats[:, 1, :], ALU.mult))
    link(nc.vector.tensor_tensor(stats[:, 0, :], stats[:, 0, :], stats[:, 2, :], ALU.add))
    link(nc.vector.tensor_scalar(stats[:, 1, :], stats[:, 0, :], 0.5, None, ALU.mult))
    link(nc.vector.reciprocal(stats[:, 2, :], stats[:, 1, :]))


ATTENTION = Steps([("x_turn", 0, c) for c in range(4)] + [("qkv", 0, c) for c in range(8)]
                  + [("qk_turn", k, c) for c in range(4) for k in range(2)]
                  + [("scores", 0, c) for c in range(4)] + [("attend", 0, c) for c in range(2)])
ROUTING = Steps([("y_turn", 0, c) for c in range(4)] + [("gate", 0, c) for c in range(4)]
                + [("s_turn", 0, c) for c in range(4)])


def attention(nc, slots, ident, h2, h_dram, wqkv, k_rope, k_decay):
    with ExitStack() as ctx:
        def sb(name, shape, dt=F32):
            return ctx.enter_context(nc.sbuf_tensor(name, shape, dt))

        def sem(name):
            return ctx.enter_context(nc.semaphore(name))

        h = sb("at_h", [128, TILES, D])
        centred = sb("at_centred", [128, TILES, D])
        squares = sb("at_squares", [128, TILES, D])
        normed = sb("at_normed", [128, TILES, D])
        stats = sb("at_stats", [128, 3, TILES])
        w = sb("at_w", [D, 3 * D])
        rope = sb("at_rope", [128, 4, D])
        decay = sb("at_decay", [128, 128])
        normed_t = sb("at_normed_t", [D, TOKENS])
        qkv = sb("at_qkv", [128, TILES, 3 * D])
        turned = sb("at_turned", [128, 2, TILES, D])
        qk_t = sb("at_qk_t", [D, 2, TOKENS])
        ret_t = sb("at_ret_t", [128, TILES, 128])

        h_in = sem("at_h_in")
        weights_in = sem("at_weights_in")
        chain = sem("at_chain")
        norm_done = sem("at_norm_done")
        variance_done = sem("at_variance_done")
        root_done = sem("at_root_done")
        rope_done = sem("at_rope_done")
        filled = sem("at_filled")
        moved = {"dve": sem("at_moved_dve"), "act": sem("at_moved_act")}
        block = ctx.enter_context(nc.Block())

        @block.sync
        def _(sp):
            src = h_dram.rearrange("(t b) (h s w) -> b s h t w", b=2, s=2, w=WW)
            for b in range(2):
                for s in range(2):
                    at = b * HH + s * HALF
                    sp.dma_start(h[at:at + HALF, :, :], src[b, s]).then_inc(h_in, 16)
            sp.dma_start(w[:], wqkv).then_inc(weights_in, 16)
            sp.dma_start(flat(rope[:]), k_rope).then_inc(weights_in, 16)
            sp.dma_start(decay[:], k_decay).then_inc(weights_in, 16)

        @block.tensor
        def _(pe):
            pe.wait_ge(weights_in, 48)
            for k, (stage, q, i) in enumerate(ATTENTION.steps):
                s = slots[:, k % SLOTS, :]
                if k >= SLOTS:
                    e, n = ATTENTION.moved_at(k - SLOTS)
                    pe.wait_ge(moved[e], n)
                if (stage, i) == ("x_turn", 0):
                    pe.wait_ge(norm_done, 1)
                if (stage, i) == ("qkv", 0):
                    for e, n in ATTENTION.outputs_of("x_turn", 0):
                        pe.wait_ge(moved[e], n)
                if (stage, i) == ("qk_turn", 0):
                    pe.wait_ge(rope_done, q + 1)
                if (stage, i) == ("scores", 0):
                    for part in range(2):
                        for e, n in ATTENTION.outputs_of("qk_turn", part):
                            pe.wait_ge(moved[e], n)
                if (stage, i) == ("attend", 0):
                    for e, n in ATTENTION.outputs_of("scores", 0):
                        pe.wait_ge(moved[e], n)
                if stage == "x_turn":
                    for j in range(8):
                        mm = nc.tensor.transpose(s[0:D, j * 128:(j + 1) * 128],
                                                 normed[:, 8 * i + j, :], ident[:, :])
                elif stage == "qkv":
                    for j in range(4):
                        at = (4 * i + j) * 128
                        mm = nc.tensor.matmul(s[:, j * 256:j * 256 + 3 * D], normed_t[:, at:at + 128],
                                              w[:, :], start=True, stop=True)
                elif stage == "qk_turn":
                    for j in range(8):
                        mm = nc.tensor.transpose(s[0:D, j * 128:(j + 1) * 128],
                                                 turned[:, q, 8 * i + j, :], ident[:, :])
                elif stage == "scores":
                    for j in range(8):
                        at = (8 * i + j) * 128
                        mm = nc.tensor.matmul(s[:, j * 128:(j + 1) * 128], qk_t[:, 1, at:at + 128],
                                              qk_t[:, 0, at:at + 128], start=True, stop=True)
                else:
                    for j in range(16):
                        t = 16 * i + j
                        mm = nc.tensor.matmul(s[:, j * D:(j + 1) * D], ret_t[:, t, :],
                                              qkv[:, t, 2 * D:3 * D], start=True, stop=True)
                mm.then_inc(filled, 1)

        def mover_program(engine, eng):
            for k, (stage, q, i) in enumerate(ATTENTION.steps):
                if ATTENTION.by[k] != engine:
                    continue
                s = slots[:, k % SLOTS, :]
                if engine == "dve" and (stage, q, i) == ("qk_turn", 0, 0):
                    rotate(eng)
                eng.wait_ge(filled, k + 1)
                if stage == "x_turn":
                    dst, src = normed_t[:, i * SLOT:(i + 1) * SLOT], s[0:D, :]
                elif stage == "qkv":
                    dst = qkv[:, 4 * i:4 * i + 4, :]
                    src = s.rearrange("p (t n) -> p t n", t=4)[:, :, 0:3 * D]
                elif stage == "qk_turn":
                    dst, src = qk_t[:, q, i * SLOT:(i + 1) * SLOT], s[0:D, :]
                if stage == "scores":
                    ins = nc.vector.tensor_tensor(ret_t[:, 8 * i:8 * i + 8, :],
                                                  s.rearrange("p (t n) -> p t n", t=8),
                                                  across(decay[:, :], 8), ALU.mult)
                elif stage == "attend":
                    ins = nc.vector.tensor_tensor(h2[:, 16 * i:16 * i + 16, :],
                                                  s.rearrange("p (t n) -> p t n", n=D),
                                                  h[:, 16 * i:16 * i + 16, :], ALU.add)
                elif engine == "dve":
                    ins = nc.vector.tensor_copy(dst, src)
                else:
                    ins = nc.scalar.copy(dst, src)
                ins.then_inc(moved[engine], 1)

        steps = [0]

        def rotate(dve):
            for e, n in ATTENTION.outputs_of("qkv", 0):
                dve.wait_ge(moved[e], n)
            for k in range(2):
                src = qkv[:, :, k * D:(k + 1) * D]
                cos, sin = rope[:, 2 * k, :], rope[:, 2 * k + 1, :]
                nc.vector.tensor_tensor(centred[:], src, across(cos, TILES), ALU.mult)
                swapped = squares[:].rearrange("p t (i r) -> p t i r", r=2)
                pairs = src.rearrange("p t (i r) -> p t i r", r=2)
                for r in range(2):
                    table = sin.rearrange("p (i r) -> p i r", r=2)[:, :, r]
                    steps[0] += 1
                    nc.vector.tensor_tensor(swapped[:, :, :, r], pairs[:, :, :, 1 - r],
                                            across(table, TILES), ALU.mult).then_inc(chain, 1)
                dve.wait_ge(chain, steps[0])
                nc.vector.tensor_tensor(turned[:, k, :, :], centred[:], squares[:],
                                        ALU.add).then_inc(rope_done, 1)
                dve.wait_ge(rope_done, k + 1)

        @block.vector
        def _(dve):
            def link(ins):
                steps[0] += 1
                ins.then_inc(chain, 1)
                dve.wait_ge(chain, steps[0])

            dve.wait_ge(h_in, 64)
            dve.wait_ge(weights_in, 48)
            centre(nc, link, h[:], centred[:], squares[:], stats).then_inc(variance_done, 1)
            dve.wait_ge(root_done, 1)
            invert_root(nc, link, stats)
            nc.vector.tensor_tensor(normed[:], centred[:], along(stats[:, 2, :], D),
                                    ALU.mult).then_inc(norm_done, 1)
            dve.wait_ge(norm_done, 1)
            mover_program("dve", dve)

        @block.scalar
        def _(act):
            act.wait_ge(variance_done, 1)
            root(nc, stats).then_inc(root_done, 1)
            mover_program("act", act)


def experts(nc, slots, ident, h2, gate_t, lattice, out_wt, out_b, ln_g, ln_b, k_select, out):
    with ExitStack() as ctx:
        def sb(name, shape, dt=F32):
            return ctx.enter_context(nc.sbuf_tensor(name, shape, dt))

        def sem(name):
            return ctx.enter_context(nc.semaphore(name))

        EB = EXPERTS // 2
        PB = 3
        y2 = sb("ex_y2", [128, TILES, 2, D])
        centred = sb("ex_centred", [128, TILES, D])
        squares = sb("ex_squares", [128, TILES, D])
        stats = sb("ex_stats", [128, 3, TILES])
        gate_w = sb("ex_gate_w", [128, PAD_N])
        lattice_w = sb("ex_lattice_w", [128, EB, D])
        out_w = sb("ex_out_w", [128, D])
        vectors = sb("ex_vectors", [128, 3, D])
        y_t = sb("ex_y_t", [128, TOKENS])
        logits = sb("ex_logits", [128, TILES, EXPERTS])
        top = sb("ex_top", [128, TILES, 8])
        above = sb("ex_above", [128, TILES, EXPERTS])
        level = sb("ex_level", [128, TILES, EXPERTS])
        run = sb("ex_run", [128, 2, TILES, EXPERTS])
        halves = sb("ex_halves", [128, TILES, 2, EXPERTS])
        halves_t = sb("ex_halves_t", [128, TOKENS], F32R)
        select = sb("ex_select", [128, EB * 128], F32R)
        weighted = sb("ex_weighted", [128, PB, SLOT])
        mixed = sb("ex_mixed", [128, 4, 512])

        weights_in = sem("ex_weights_in")
        zeroed = sem("ex_zeroed")
        chain = sem("ex_chain")
        norm_done = sem("ex_norm_done")
        variance_done = sem("ex_variance_done")
        root_done = sem("ex_root_done")
        copied = sem("ex_copied")
        shifted = sem("ex_shifted")
        exp_done = sem("ex_exp_done")
        halves_done = sem("ex_halves_done")
        filled = sem("ex_filled")
        moved = {"dve": sem("ex_moved_dve"), "act": sem("ex_moved_act")}
        spread = sem("ex_spread")
        weigh = sem("ex_weigh")
        summed = sem("ex_summed")
        mixed_out = sem("ex_mixed_out")
        projected = sem("ex_projected")
        result = sem("ex_result")
        stored = sem("ex_stored")
        block = ctx.enter_context(nc.Block())
        select_raw = y2[:].rearrange("p t a d -> p (t a d)")

        @block.sync
        def _(sp):
            sp.dma_start(select_raw, k_select).then_inc(weights_in, 16)
            sp.dma_start(flat(lattice_w[:]), lattice).then_inc(weights_in, 16)
            for half in range(2):
                sp.dma_start(out_w[half * D:(half + 1) * D, :], out_wt).then_inc(weights_in, 16)
            for n, v in enumerate((out_b, ln_g, ln_b)):
                sp.dma_start(vectors[:, n, :], v.rearrange("(a d) -> a d", a=1).broadcast_to(
                    [128, D])).then_inc(weights_in, 16)
            sp.wait_ge(zeroed, 1)
            sp.dma_start(gate_w[0:D, 0:EXPERTS], gate_t).then_inc(weights_in, 16)
            sp.wait_ge(result, 1)
            sp.dma_start(out.rearrange("(t b) h w -> (b h) t w", b=2), squares[:]).then_inc(stored, 16)
            sp.wait_ge(stored, 16)

        @block.tensor
        def _(pe):
            pe.wait_ge(weights_in, 128)
            for k, (stage, q, i) in enumerate(ROUTING.steps):
                s = slots[:, k % SLOTS, :]
                if k >= SLOTS:
                    e, n = ROUTING.moved_at(k - SLOTS)
                    pe.wait_ge(moved[e], n)
                if (stage, i) == ("y_turn", 0):
                    pe.wait_ge(norm_done, 1)
                    pe.wait_ge(copied, 1)
                if (stage, i) == ("gate", 0):
                    for e, n in ROUTING.outputs_of("y_turn", 0):
                        pe.wait_ge(moved[e], n)
                if (stage, i) == ("s_turn", 0):
                    pe.wait_ge(halves_done, 1)
                for j in range(8):
                    t = 8 * i + j
                    if stage == "gate":
                        mm = nc.tensor.matmul(s[:, j * 128:j * 128 + PAD_N], y_t[:, t * 128:(t + 1) * 128],
                                              gate_w[:, :], start=True, stop=True)
                    else:
                        src = y2 if stage == "y_turn" else halves
                        mm = nc.tensor.transpose(s[:, j * 128:(j + 1) * 128], flat(src[:, t, :, :]),
                                                 ident[:, :])
                mm.then_inc(filled, 1)
            for e in moved:
                pe.wait_ge(moved[e], ROUTING.moved[e])
            with pe.Fori(0, 4) as g:
                def spread_block(n):
                    if n >= PB:
                        pe.wait_ge(weigh, g * EB + (n - PB + 1))
                    for j in range(2):
                        mm = nc.tensor.matmul(slots[:, n % PB, j * 512:(j + 1) * 512],
                                              select[:, n * 128:(n + 1) * 128],
                                              halves_t[:, bass.ds(g * SLOT + j * 512, 512)],
                                              start=True, stop=True)
                    mm.then_inc(spread, 1)

                for n in range(PB - 1):
                    spread_block(n)
                for n in range(EB):
                    if n + PB - 1 < EB:
                        spread_block(n + PB - 1)
                    pe.wait_ge(weigh, g * EB + (n + 1))
                    for j in range(2):
                        mm = nc.tensor.matmul(slots[j * D:(j + 1) * D, SLOTS - 1, 0:512],
                                              lattice_w[:, n, :], weighted[:, n % PB, j * 512:(j + 1) * 512],
                                              start=(n == 0), stop=(n == EB - 1))
                mm.then_inc(summed, 1)
                pe.wait_ge(mixed_out, g + 1)
            for i in range(2):
                for j in range(16):
                    t = 16 * i + j
                    half = t % 8 // 4
                    rows = slice(half * D, half * D + D)
                    at = t % 4 * 128
                    to = half * 512 + (j // 8 * 4 + t % 4) * D
                    mm = nc.tensor.matmul(slots[:, i, to:to + D], mixed[rows, t // 8, at:at + 128],
                                          out_w[rows, :], start=True, stop=True)
                mm.then_inc(projected, 1)

        def mover_program(engine, eng):
            for k, (stage, q, i) in enumerate(ROUTING.steps):
                if engine == "dve" and (stage, i) == ("s_turn", 0):
                    route(eng)
                if engine == "act" and (stage, i) == ("s_turn", 0):
                    eng.wait_ge(shifted, 1)
                    nc.scalar.activation(level[:], level[:], ACT.Exp).then_inc(exp_done, 1)
                if ROUTING.by[k] != engine:
                    continue
                s = slots[:, k % SLOTS, :]
                eng.wait_ge(filled, k + 1)
                if stage == "gate":
                    dst = logits[:, 8 * i:8 * i + 8, :]
                    src = s.rearrange("p (t n) -> p t n", t=8)[:, :, 0:EXPERTS]
                else:
                    dst = (y_t if stage == "y_turn" else halves_t)[:, i * SLOT:(i + 1) * SLOT]
                    src = s
                if engine == "dve":
                    nc.vector.tensor_copy(dst, src).then_inc(moved[engine], 1)
                else:
                    nc.scalar.copy(dst, src).then_inc(moved[engine], 1)

        steps = [0]

        def linked(dve):
            def link(ins):
                steps[0] += 1
                ins.then_inc(chain, 1)
                dve.wait_ge(chain, steps[0])
            return link

        def route(dve):
            link = linked(dve)
            for e, n in ROUTING.outputs_of("gate", 0):
                dve.wait_ge(moved[e], n)
            for t in range(TILES):
                last = nc.vector.max(top[:, t, :], logits[:, t, :])
            link(last)
            least, most = top[:, :, TOP_K - 1], top[:, :, 0]
            nc.vector.tensor_tensor(level[:], logits[:], along(most, EXPERTS),
                                    ALU.subtract).then_inc(shifted, 1)
            nc.vector.tensor_tensor(run[:, 0], logits[:], along(least, EXPERTS), ALU.is_equal)
            link(nc.vector.tensor_tensor(above[:], logits[:], along(least, EXPERTS), ALU.is_gt))
            nc.vector.tensor_copy(squares[:], run[:, 0])
            link(nc.vector.tensor_reduce(stats[:, 0, :], above[:], AX_X, ALU.add))
            link(nc.vector.tensor_scalar(stats[:, 1, :], stats[:, 0, :], -1.0, float(TOP_K),
                                         ALU.mult, ALU.add))
            shift, at = 1, 0
            while shift < EXPERTS:
                nc.vector.tensor_copy(run[:, 1 - at, :, 0:shift], run[:, at, :, 0:shift])
                link(nc.vector.tensor_tensor(run[:, 1 - at, :, shift:], run[:, at, :, shift:],
                                             run[:, at, :, 0:EXPERTS - shift], ALU.add))
                shift, at = 2 * shift, 1 - at
            link(nc.vector.tensor_tensor(run[:, 1 - at], run[:, at], along(stats[:, 1, :], EXPERTS),
                                         ALU.is_le))
            link(nc.vector.tensor_tensor(run[:, at], run[:, 1 - at], squares[:], ALU.mult))
            link(nc.vector.tensor_tensor(above[:], above[:], run[:, at], ALU.add))
            dve.wait_ge(exp_done, 1)
            link(nc.vector.tensor_tensor(squares[:], level[:], above[:], ALU.mult))
            link(nc.vector.tensor_reduce(stats[:, 0, :], squares[:], AX_X, ALU.add))
            link(nc.vector.reciprocal(stats[:, 1, :], stats[:, 0, :]))
            link(nc.vector.tensor_tensor(level[:], squares[:], along(stats[:, 1, :], EXPERTS), ALU.mult))
            link(nc.vector.tensor_copy(halves[:, :, 0, :].bitcast(F32R), level[:]))
            nc.vector.tensor_tensor(halves[:, :, 1, :], level[:], halves[:, :, 0, :],
                                    ALU.subtract).then_inc(halves_done, 1)

        @block.vector
        def _(dve):
            link = linked(dve)
            nc.vector.memset(gate_w[:], 0.0).then_inc(zeroed, 1)
            dve.wait_ge(weights_in, 128)
            link(nc.vector.tensor_copy(select[:], select_raw))
            centre(nc, link, h2[:], centred[:], squares[:], stats).then_inc(variance_done, 1)
            dve.wait_ge(root_done, 1)
            invert_root(nc, link, stats)
            nc.vector.tensor_tensor(y2[:, :, 0, :], centred[:], along(stats[:, 2, :], D),
                                    ALU.mult).then_inc(norm_done, 1)
            mover_program("dve", dve)
            for e in moved:
                dve.wait_ge(moved[e], ROUTING.moved[e])
            with dve.Fori(0, 4) as g:
                for n in range(EB):
                    dve.wait_ge(spread, g * EB + (n + 1))
                    nc.vector.tensor_tensor(weighted[:, n % PB, :], slots[:, n % PB, :],
                                            y_t[:, bass.ds(g * SLOT, SLOT)], ALU.mult).then_inc(weigh, 1)
            nc.vector.tensor_tensor(level[:], y2[:, :, 0, :], across(vectors[:, 0, :], TILES),
                                    ALU.add).then_inc(chain, 1)
            steps[0] += 1
            dve.wait_ge(chain, steps[0])
            for i in range(2):
                dve.wait_ge(projected, i + 1)
                part = level[:, 16 * i:16 * i + 16, :].rearrange("p (a h t) d -> p a h (t d)", a=2, h=2)
                link(nc.vector.tensor_tensor(
                    part, slots[:, i, :].rearrange("p (h a n) -> p a h n", a=2, h=2), part, ALU.add))
            centre(nc, link, level[:], centred[:], squares[:], stats).then_inc(variance_done, 1)
            dve.wait_ge(root_done, 2)
            invert_root(nc, link, stats)
            link(nc.vector.tensor_tensor(level[:], centred[:], along(stats[:, 2, :], D), ALU.mult))
            link(nc.vector.tensor_tensor(level[:], level[:], across(vectors[:, 1, :], TILES), ALU.mult))
            link(nc.vector.tensor_tensor(centred[:], h2[:], across(vectors[:, 2, :], TILES), ALU.add))
            nc.vector.tensor_tensor(squares[:], level[:], centred[:], ALU.add).then_inc(result, 1)

        @block.scalar
        def _(act):
            act.wait_ge(variance_done, 1)
            root(nc, stats).then_inc(root_done, 1)
            act.wait_ge(norm_done, 1)
            nc.scalar.copy(y2[:, :, 1, :], y2[:, :, 0, :]).then_inc(copied, 1)
            mover_program("act", act)
            with act.Fori(0, 4) as g:
                act.wait_ge(summed, g + 1)
                nc.scalar.copy(mixed[:, bass.ds(g, 1), :].rearrange("p a n -> p (a n)"),
                               slots[:, SLOTS - 1, 0:512]).then_inc(mixed_out, 1)
            act.wait_ge(variance_done, 2)
            root(nc, stats).then_inc(root_done, 1)


def build(nc, x, fc0_w, fc0_b, sw, cwt, cb, fc1_w, fc1_b, fc2_w, fc2_b, wqkv, gate_t, lattice,
          out_wt, out_b, ln_g, ln_b, k_fwd_w, k_fwd_h, k_inv_h, k_inv_w, k_rope, k_decay, k_select,
          k_ident, out):
    h_dram = nc.dram_tensor("h_scratch", (IMAGES, SPATIAL), F32, kind="Internal").ap()
    with (
        nc.psum_tensor("slots", [128, SLOTS, SLOT], F32) as slots,
        nc.sbuf_tensor("ident", [128, 128], F32) as ident,
        nc.semaphore("ident_in") as ident_in,
    ):
        nc.sync.dma_start(ident[:, :], k_ident).then_inc(ident_in, 16)
        tower(nc, slots, ident, ident_in, h_dram, x, fc0_w, fc0_b, sw, cwt, cb, fc1_w, fc1_b, fc2_w,
              fc2_b, k_fwd_w, k_fwd_h, k_inv_h, k_inv_w)
        with nc.sbuf_tensor("h2", [128, TILES, D], F32) as h2:
            attention(nc, slots, ident, h2, h_dram, wqkv, k_rope, k_decay)
            experts(nc, slots, ident, h2, gate_t, lattice, out_wt, out_b, ln_g, ln_b, k_select, out)


def kernel(**inputs):
    import numpy as _np
    import concourse.bacc as _bacc
    from concourse import mybir as _mybir
    from concourse.bass_utils import run_bass_kernel_spmd as _run

    f = {n: _np.asarray(a) for n, a in inputs.items()}
    t = "L0_tok_"
    order = [(n + 1) % LAYERS for n in range(LAYERS)]
    sw = _np.stack([f[f"{t}sw{n}"] for n in order])
    sw = sw.reshape(LAYERS, CH, CH, MODES, KY_BLOCKS, 4).transpose(0, 5, 1, 4, 3, 2)
    wq, wk = f["L0_attn_W_Q"], f["L0_attn_W_K"]
    fwd_w, fwd_h, inv_h, inv_w = dft_constants()
    rope, decay, select = attention_constants()
    arrays = {
        "x": f["x"].reshape(GROUPS, GB, 2, HALF, WW, 3).transpose(0, 1, 5, 3, 2, 4).reshape(
            GROUPS, 3 * GB, SPATIAL),
        "fc0_w": f[t + "fc0_w"], "fc0_b": f[t + "fc0_b"],
        "sw": sw.reshape(LAYERS, 128, KY_BLOCKS * MODES * CH),
        "cwt": _np.stack([f[f"{t}cw{n}"].T for n in range(LAYERS)]),
        "cb": _np.stack([f[f"{t}cb{n}"] for n in range(LAYERS)], axis=1),
        "fc1_w": f[t + "fc1_w"], "fc1_b": f[t + "fc1_b"],
        "fc2_w": f[t + "fc2_w"], "fc2_b": f[t + "fc2_b"],
        "wqkv": _np.concatenate([wq, wk, f["L0_attn_W_V"]], axis=1),
        "gate_t": f["L0_ffn_gate_w"].T,
        "lattice": f["L0_ffn_lattice_weights"].reshape(EXPERTS // 2, 2, D, D).transpose(1, 2, 0, 3).reshape(128, -1),
        "out_wt": f["L0_ffn_out_w"].T, "out_b": f["L0_ffn_out_b"],
        "ln_g": f["L0_ffn_ln_g"], "ln_b": f["L0_ffn_ln_b"],
        "k_fwd_w": fwd_w, "k_fwd_h": fwd_h, "k_inv_h": inv_h, "k_inv_w": inv_w,
        "k_rope": rope, "k_decay": decay, "k_select": select,
        "k_ident": _np.eye(128, dtype=_np.float32),
    }
    nc = _bacc.Bacc("TRN2", target_bir_lowering=False, num_devices=1)
    arrays = {f"in_{n}_dram": _np.ascontiguousarray(a) for n, a in arrays.items()}
    args = [nc.dram_tensor(n, a.shape, _mybir.dt.from_np(a.dtype), kind="ExternalInput").ap()
            for n, a in arrays.items()]
    out = nc.dram_tensor("out_0_dram", (IMAGES, HH, WW), _mybir.dt.float32, kind="ExternalOutput").ap()
    build(nc, *args, out)
    r = _run(nc, [arrays], core_ids=[0])
    return r.results[0]["out_0_dram"]
```

```python
from contextlib import ExitStack

import numpy as np

import concourse.bass as bass
from concourse import mybir

F32 = mybir.dt.float32
F32R = mybir.dt.float32r
ALU = mybir.AluOpType
ACT = mybir.ActivationFunctionType
AX_X = mybir.AxisListType.X

IMAGES, HH, WW = 64, 64, 64
CH = 32
MODES = 20
LAYERS = 4
QB = 4
GB = 16
QUADS = GB // QB
GROUPS = IMAGES // GB
HALF = HH // 2
SPATIAL = HH * WW
PART = SPATIAL // 4
PAD_N = 96
PAD_K = 96
BLOCKS = MODES // 4
HID = 64
SLOT = 1024
SLOTS = 4
TOKENS = IMAGES * HH
TILES = TOKENS // 128
D = 64
EXPERTS = 64
TOP_K = 6
EPS = 1e-5


def dft_constants():
    k = np.arange(MODES)
    norm = 1.0 / np.sqrt(HH * WW)
    pos = np.arange(HH)
    angle = 2 * np.pi * np.outer(pos, k) / HH
    cos, sin = np.cos(angle), np.sin(angle)
    twice = np.where(k == 0, 1.0, 2.0)
    rows_fwd = np.zeros((128, PAD_N))
    cols_fwd = np.zeros((2, WW, 2, 4, 8, 2, 2))
    for part in range(128):
        a, x, r, s = part // 32, part // 16 % 2, part // 2 % 8, part % 2
        h = 32 * s + 8 * a + r
        rows_fwd[part, x * 40:x * 40 + 40:2] = norm * cos[h]
        rows_fwd[part, x * 40 + 1:x * 40 + 40:2] = -norm * sin[h]
    for y in range(2):
        for kw in range(MODES):
            m, j = kw // 4, kw % 4
            cols_fwd[y, :, 0, j, m, y, 0] = twice[kw] * cos[:, kw]
            cols_fwd[y, :, 0, j, m, y, 1] = -twice[kw] * sin[:, kw]
            cols_fwd[y, :, 1, j, m, y, 0] = twice[kw] * sin[:, kw]
            cols_fwd[y, :, 1, j, m, y, 1] = twice[kw] * cos[:, kw]
    rows_inv = np.zeros((PAD_K, 2, 2, 2, HALF))
    for y in range(2):
        for kh in range(MODES):
            at, p = 4 * kh + 2 * y, kh % 2
            rows_inv[at, y, p, 0] = cos[:HALF, kh]
            rows_inv[at + 1, y, p, 0] = -sin[:HALF, kh]
            rows_inv[at, y, p, 1] = sin[:HALF, kh]
            rows_inv[at + 1, y, p, 1] = cos[:HALF, kh]
    cols_inv = np.zeros((2, 2, 32, 2, WW))
    for p in range(2):
        for s in range(2):
            sign = -1.0 if s * p else 1.0
            cols_inv[p, 0, :MODES, s] = sign * norm * cos.T
            cols_inv[p, 1, :MODES, s] = -sign * norm * sin.T
    f32 = np.float32
    return (rows_fwd.astype(f32), cols_fwd.reshape(128, -1).astype(f32),
            rows_inv.reshape(PAD_K, -1).astype(f32), cols_inv.reshape(128, -1).astype(f32))


def attention_constants():
    f = np.float32
    gamma, scale_base = 0.96875, 512.0
    even = np.arange(0, D, 2, dtype=f)
    inv_freq = (f(1.0) / f(10000.0) ** (even / f(D))).astype(f)
    pos = np.arange(HH, dtype=f)
    ang = pos[:, None] * inv_freq[None, :]
    sin, cos = np.sin(ang), np.cos(ang)
    base = (even + f(0.4 * D)) / f(1.4 * D)
    scale = base[None, :] ** (pos[:, None] / f(scale_base))
    rope = np.zeros((128, 4, D), f)
    for k, sc in enumerate((scale, 1.0 / scale)):
        for image in range(2):
            rows = slice(image * HH, image * HH + HH)
            rope[rows, 2 * k, 0::2] = cos * sc
            rope[rows, 2 * k, 1::2] = cos * sc
            rope[rows, 2 * k + 1, 0::2] = -sin * sc
            rope[rows, 2 * k + 1, 1::2] = sin * sc
    decay = np.zeros((128, 128), f)
    for image in range(2):
        for m in range(HH):
            n = np.arange(m, HH)
            decay[image * HH + m, image * HH + n] = gamma ** (n - m)
    select = np.zeros((2, EXPERTS, EXPERTS // 2, 2, D), f)
    for e in range(EXPERTS):
        select[:, e, e // 2, e % 2, :] = 1.0
    return rope.reshape(128, -1), decay, select.reshape(128, -1)


def layer_steps():
    s = []
    for q in range(QUADS):
        for i in range(4):
            s.append(("fwd_rows", q, i))
            if i == 1 and q > 0:
                s += [("fwd_cols", q - 1, 0), ("fwd_cols", q - 1, 1)]
    s += [("fwd_cols", QUADS - 1, 0), ("fwd_cols", QUADS - 1, 1)]
    s += [("mix", 0, i) for i in range(BLOCKS)]
    s += [("modes_turn", 0, 0), ("modes_turn", 0, 1), ("modes_turn", 1, 0)]
    s += [("inv_rows", 0, i) for i in range(4)]
    s += [("modes_turn", 1, 1)]
    for q in range(QUADS):
        for i in range(4):
            s.append(("out", q, i))
            if q + 1 < QUADS:
                s.append(("inv_rows", q + 1, i))
            if q + 2 < QUADS and i % 2:
                s.append(("modes_turn", q + 2, i // 2))
    return s


def mover(stage, q, i):
    if stage in ("out", "fc1", "modes_turn"):
        return "act"
    if stage in ("fwd_rows", "mix", "fc0", "x_turn", "qkv", "y_turn", "gate", "s_turn"):
        return "act" if i % 2 else "dve"
    if stage == "qk_turn":
        return "act" if q else "dve"
    return "dve"


class Steps:

    def __init__(self, steps):
        self.steps = steps
        self.index = {s: k for k, s in enumerate(steps)}
        self.by = [mover(*s) for s in steps]
        self.count = len(steps)
        self.moved = {e: sum(b == e for b in self.by) for e in ("dve", "act")}

    def moved_at(self, k):
        return self.by[k], sum(b == self.by[k] for b in self.by[:k + 1])

    def outputs_of(self, stage, q):
        last = {}
        for k, (st, qq, _) in enumerate(self.steps):
            if (st, qq) == (stage, q):
                e, n = self.moved_at(k)
                last[e] = n
        return last.items()


def head_steps():
    s = []
    for pair in range(2 * QUADS + 1):
        for i in range(4):
            if pair < 2 * QUADS:
                s.append(("fc1", pair, i))
            if i == 1 and pair > 0:
                s.append(("fc2", pair - 1, 0))
    return s


LIFT = Steps([("fc0", q, i) for q in range(QUADS) for i in range(QB)])
LAYER = Steps(layer_steps())
HEAD = Steps(head_steps())
GROUP_FILLED = LIFT.count + LAYERS * LAYER.count + HEAD.count
GROUP_MOVED = {e: LIFT.moved[e] + LAYERS * LAYER.moved[e] + HEAD.moved[e] for e in ("dve", "act")}


def flat(t):
    names = " ".join("abcd"[:len(t.shape) - 1])
    return t.rearrange(f"p {names} -> p ({names})") if len(t.shape) > 2 else t


def across(t, n):
    return t.rearrange("p (a k) -> p a k", a=1).broadcast_to([t.shape[0], n, t.shape[1]])


def along(t, n):
    return t.rearrange("p (k a) -> p k a", a=1).broadcast_to([t.shape[0], t.shape[1], n])


def tower(nc, slots, ident, ident_in, h_dram, x, fc0_w, fc0_b, sw, cwt, cb, fc1_w, fc1_b, fc2_w, fc2_b,
          k_fwd_rows, k_fwd_cols, k_inv_rows, k_inv_cols):
    with ExitStack() as ctx:
        LB = 8

        def sb(name, shape, dt=F32):
            return ctx.enter_context(nc.sbuf_tensor(name, shape, dt))

        def sem(name):
            return ctx.enter_context(nc.semaphore(name))

        fwd_rows = sb("fwd_rows", [128, PAD_N])
        fwd_cols = sb("fwd_cols", [128, 2, 128])
        inv_rows = sb("inv_rows", [PAD_K, 2, 128])
        inv_cols = sb("inv_cols", [128, 128])
        lift_w = sb("lift_w", [PAD_K, LB, 128])
        lift_b = sb("lift_b", [128, 1])
        conv_all = sb("conv_all", [128, LAYERS, 128])
        conv_w = sb("conv_w", [128, 128])
        conv_b_all = sb("conv_b_all", [128, LAYERS])
        conv_b = sb("conv_b", [128, 1])
        w1 = sb("w1", [128, 2, 128])
        b1 = sb("b1", [128, 1])
        w2 = sb("w2", [128, 32])
        b2 = sb("b2", [128, 1])
        mode_w = sb("mode_w", [128, BLOCKS * MODES, CH])

        xin = sb("xin", [PAD_K, 2, PART])
        act_c = sb("act_c", [128, QUADS, QB, PART])
        big = sb("big", [128, 2, SPATIAL])
        mid = sb("mid", [128, 2, 2, 2, MODES, CH])
        modes = sb("modes", [128, 8, 2 * QUADS, 4 * MODES])
        modes_t = sb("modes_t", [PAD_K, 2, 2, MODES * CH])
        rows = sb("rows", [128, 2, SLOT])

        filled = sem("filled")
        moved = {"dve": sem("moved_dve"), "act": sem("moved_act")}
        const_in = sem("const_in")
        zeroed = sem("zeroed")
        x_in = sem("x_in")
        mode_w_in = sem("mode_w_in")
        conv_w_set = sem("conv_w_set")
        turned = sem("turned")
        mix_started = sem("mix_started")
        h_out = [sem(f"h_out{b}") for b in range(2)]

        plain = [(fwd_rows, k_fwd_rows), (fwd_cols, k_fwd_cols), (inv_rows, k_inv_rows),
                 (inv_cols, k_inv_cols)]
        blocks = [(lift_w[12 * b + 3 * a:12 * b + 3 * a + 3, b, a * CH:(a + 1) * CH], fc0_w)
                  for b in range(LB) for a in range(4)]
        blocks += [(conv_all[b * CH:(b + 1) * CH, :, b * CH:(b + 1) * CH],
                    cwt.rearrange("l c o -> c l o")) for b in range(QB)]
        blocks += [(w1[b * CH:(b + 1) * CH, b // 2, (b % 2) * HID:(b % 2 + 1) * HID], fc1_w)
                   for b in range(QB)]
        blocks += [(w2[b * HID:(b + 1) * HID, b:b + 1], fc2_w) for b in range(2)]
        columns = [(lift_b[b * CH:(b + 1) * CH, :], fc0_b.rearrange("(c a) -> c a", a=1))
                   for b in range(QB)]
        columns += [(conv_b_all[b * CH:(b + 1) * CH, :], cb)
                    for b in range(QB)]
        columns += [(b1[b * HID:(b + 1) * HID, :], fc1_b.rearrange("(c a) -> c a", a=1))
                    for b in range(2)]
        columns += [(b2[:, :], fc2_b.rearrange("(a c) -> a c", a=1).broadcast_to([128, 1]))]
        CONSTS = 16 * (len(plain) + len(blocks) + len(columns))

        TURNS = 2 * QUADS * LAYERS + 2
        block = ctx.enter_context(nc.Block())

        @block.sync
        def _(sp):
            for dst, src in plain:
                sp.dma_start(flat(dst[:]), src).then_inc(const_in, 16)
            sp.dma_start(flat(mode_w[:]), sw[LAYERS - 1]).then_inc(mode_w_in, 16)
            sp.wait_ge(zeroed, 1)
            for dst, src in blocks + columns:
                sp.dma_start(dst, src).then_inc(const_in, 16)
            with sp.Fori(0, GROUPS) as g:
                sp.dma_start(xin[:], x[g].rearrange("(n p) m -> p n m", n=2)).then_inc(x_in, 16)
                with sp.Fori(0, LAYERS) as l:
                    start = g * GROUP_FILLED + LIFT.count + l * LAYER.count
                    sp.wait_ge(filled, start + (LAYER.index["mix", 0, BLOCKS - 1] + 1))
                    sp.dma_start(flat(mode_w[:]), sw[l]).then_inc(mode_w_in, 16)
                for pair in range(2 * QUADS):
                    _, n = HEAD.moved_at(HEAD.index["fc2", pair, 0])
                    sp.wait_ge(moved["dve"], g * GROUP_MOVED["dve"] + (
                        LIFT.moved["dve"] + LAYERS * LAYER.moved["dve"] + n))
                    for a in range(2):
                        dst = h_dram.rearrange("(g n) b m -> g n b m", g=GROUPS)[g, 2 * pair + a]
                        sp.dma_start(dst, rows[a:128:32, pair % 2, :]).then_inc(h_out[pair % 2], 16)
            for b in range(2):
                sp.wait_ge(h_out[b], 16 * IMAGES // 2)
            sp.wait_ge(mode_w_in, 16 * (1 + GROUPS * LAYERS))

        def slot_of(k):
            return slots[:, k % SLOTS, :]

        def lift_pe(k, q, i):
            b = QB * q + i
            for j in range(2):
                mm = nc.tensor.matmul(slot_of(k)[:, j * 512:(j + 1) * 512], lift_w[:, b % LB, :],
                                      xin[:, b // LB, j * 512:(j + 1) * 512], start=True, stop=True)
            return mm

        def layer_pe(k, stage, q, i):
            s = slot_of(k)
            if stage == "fwd_rows":
                xt = big[:, q % 2, :].rearrange("p (c m) -> p c m", c=CH)
                for j in range(8):
                    mm = nc.tensor.matmul(s[:, j * 128:j * 128 + PAD_N], xt[:, 8 * i + j, :],
                                          fwd_rows[:, :], start=True, stop=True)
            elif stage == "fwd_cols":
                for lo, hi in ((0, 512), (512, MODES * CH)):
                    for r in range(2):
                        src = mid[:, q % 2, r, i, :, :].rearrange("p k c -> p (k c)")
                        mm = nc.tensor.matmul(s[:, lo:hi], fwd_cols[:, r, :], src[:, lo:hi],
                                              start=(r == 0), stop=(r == 1))
            elif stage == "mix":
                for kh in range(MODES):
                    for j in range(4):
                        rows_j = slice(j * CH, (j + 1) * CH)
                        mm = nc.tensor.matmul(s[rows_j, kh * 32:(kh + 1) * 32],
                                              mode_w[rows_j, i * MODES + kh, :],
                                              modes[rows_j, i, :, 4 * kh:4 * kh + 4],
                                              start=True, stop=True)
            elif stage == "modes_turn":
                for kb in range(BLOCKS):
                    mm = nc.tensor.transpose(s[0:4 * MODES, kb * 128:(kb + 1) * 128],
                                             modes[:, kb, 2 * q + i, :], ident[:, :])
            elif stage == "inv_rows":
                for lo, hi in ((0, 512), (512, MODES * CH)):
                    mm = nc.tensor.matmul(s[:, lo:hi], inv_rows[:, i // 2, :],
                                          modes_t[:, q % 2, i % 2, lo:hi], start=True, stop=True)
            elif stage == "out":
                v = big[:, q % 2, :].rearrange("p (b r m) -> p b r m", b=QB, r=8)
                for j in range(2):
                    nc.tensor.matmul(s[:, j * 512:(j + 1) * 512], conv_w[:, :],
                                     act_c[:, q, i, j * 512:(j + 1) * 512],
                                     start=True, stop=False, skip_group_check=True)
                    for h in range(4):
                        r = 4 * j + h
                        mm = nc.tensor.matmul(s[:, r * 128:(r + 1) * 128], v[:, i, r, :], inv_cols[:, :],
                                              start=False, stop=(h == 3), skip_group_check=True)
            return mm

        def head_pe(k, stage, pair, i):
            s = slot_of(k)
            if stage == "fc1":
                for j in range(2):
                    mm = nc.tensor.matmul(s[:, j * 512:(j + 1) * 512], w1[:, pair % 2, :],
                                          act_c[:, pair // 2, i, j * 512:(j + 1) * 512],
                                          start=True, stop=True)
            else:
                for u in range(2):
                    for b in range(QB):
                        at = b * PART + u * 512
                        mm = nc.tensor.matmul(s[32 * b:32 * b + 32, u * 512:(u + 1) * 512], w2[:, :],
                                              big[:, pair % 2, at:at + 512], start=True, stop=True)
            return mm

        READS = {"fwd_cols": "fwd_rows", "modes_turn": "mix"}

        @block.tensor
        def _(pe):
            pe.wait_ge(const_in, CONSTS)
            pe.wait_ge(ident_in, 16)
            with pe.Fori(0, GROUPS) as g:
                at = {e: g * GROUP_MOVED[e] for e in moved}
                pe.wait_ge(x_in, g * 16 + 16)
                for k, (stage, q, i) in enumerate(LIFT.steps):
                    if k >= SLOTS:
                        e, n = LIFT.moved_at(k - SLOTS)
                        pe.wait_ge(moved[e], at[e] + n)
                    lift_pe(k, q, i).then_inc(filled, 1)
                with pe.Fori(0, LAYERS) as l:
                    at = {e: g * GROUP_MOVED[e] + l * LAYER.moved[e] for e in moved}
                    for e in moved:
                        pe.wait_ge(moved[e], at[e] + LIFT.moved[e])
                    for k, (stage, q, i) in enumerate(LAYER.steps):
                        if k >= SLOTS:
                            e, n = LAYER.moved_at(k - SLOTS)
                            pe.wait_ge(moved[e], at[e] + (LIFT.moved[e] + n))
                        if stage in READS and i == 0:
                            for e, n in LAYER.outputs_of(READS[stage], 0 if stage == "modes_turn" else q):
                                pe.wait_ge(moved[e], at[e] + (LIFT.moved[e] + n))
                        if stage == "fwd_rows" and i == 0:
                            pe.wait_ge(turned, g * TURNS + (l * (2 * QUADS) + (2 * q + 2)))
                        if stage == "inv_rows":
                            e, n = LAYER.moved_at(LAYER.index["modes_turn", q, i % 2])
                            pe.wait_ge(moved[e], at[e] + (LIFT.moved[e] + n))
                        if stage == "out":
                            e, n = LAYER.moved_at(LAYER.index["inv_rows", q, i])
                            pe.wait_ge(moved[e], at[e] + (LIFT.moved[e] + n))
                        if stage == "mix" and i == 0:
                            for e, n in LAYER.outputs_of("fwd_cols", QUADS - 1):
                                pe.wait_ge(moved[e], at[e] + (LIFT.moved[e] + n))
                            pe.wait_ge(mode_w_in, g * (16 * LAYERS) + (l * 16 + 16))
                        if (stage, q, i) == ("out", 0, 0):
                            pe.wait_ge(conv_w_set, g * (2 * LAYERS) + (l * 2 + 2))
                        if stage == "mix":
                            pe.sem_inc(mix_started, 1)
                        layer_pe(k, stage, q, i).then_inc(filled, 1)
                base = {e: LIFT.moved[e] + LAYERS * LAYER.moved[e] for e in moved}
                at = {e: g * GROUP_MOVED[e] for e in moved}
                for e in moved:
                    pe.wait_ge(moved[e], at[e] + base[e])
                pe.wait_ge(turned, g * TURNS + TURNS)
                for k, (stage, pair, i) in enumerate(HEAD.steps):
                    if k >= SLOTS:
                        e, n = HEAD.moved_at(k - SLOTS)
                        pe.wait_ge(moved[e], at[e] + (base[e] + n))
                    if stage == "fc2":
                        for e, n in HEAD.outputs_of("fc1", pair):
                            pe.wait_ge(moved[e], at[e] + (base[e] + n))
                    head_pe(k, stage, pair, i).then_inc(filled, 1)
                for e in moved:
                    pe.wait_ge(moved[e], at[e] + (base[e] + HEAD.moved[e]))

        def plain_move(engine, dst, src):
            if engine == "dve":
                return nc.vector.tensor_copy(dst, src)
            return nc.scalar.copy(dst, src)

        def biased_move(engine, dst, src, bias):
            if engine == "dve":
                return nc.vector.tensor_scalar(dst, src, bias, None, ALU.add)
            return nc.scalar.activation(dst, src, ACT.Identity, bias=bias)

        def move(engine, k, stage, q, i, l=None):
            s = slot_of(k)
            if stage == "fc0":
                dst = act_c[:, q, i, :]
                return biased_move(engine, dst, s, lift_b[:, 0:1])
            if stage == "fwd_rows":
                dst = mid[:, q % 2, :, :, :, 8 * i:8 * i + 8].rearrange("p r x k c -> p c (x k) r")
                src = s.rearrange("p (c n) -> p c n", c=8)[:, :, 0:4 * MODES]
                return plain_move(engine, dst, src.rearrange("p c (k r) -> p c k r", r=2))
            if stage == "fwd_cols":
                dst = modes[:, :, 2 * q + i, :].rearrange("p m (k b) -> p k m b", b=4)
                return nc.vector.transpose(dst, s[:, 0:MODES * CH])
            if stage == "mix":
                dst = modes[:, i, :, :].rearrange("p q (k b) -> p k q b", b=4)
                return plain_move(engine, dst, s[:, 0:MODES * 32].rearrange(
                    "p (k q b) -> p k q b", k=MODES, b=4))
            if stage == "modes_turn":
                return plain_move(engine, modes_t[0:4 * MODES, q % 2, i, :],
                                  s[0:4 * MODES, 0:MODES * CH])
            if stage == "inv_rows":
                dst = big[:, q % 2, i * PART:(i + 1) * PART].rearrange("p (r a o) -> p o a r", r=8, a=4)
                return nc.vector.transpose(dst, s.rearrange("p (k o) -> p o k", o=CH))
            if stage == "out":
                return nc.scalar.activation(act_c[:, q, i, :], s, ACT.Gelu,
                                            bias=conv_b[:, 0:1])
            if stage == "fc1":
                return nc.scalar.activation(big[:, q % 2, i * SLOT:(i + 1) * SLOT], s, ACT.Gelu,
                                            bias=b1[:, 0:1])
            if stage == "fc2":
                return nc.vector.tensor_scalar(rows[:, q % 2, :], s, b2[:, 0:1], None, ALU.add)

        def turn(q, y):
            src = act_c[:, q, 2 * y:2 * y + 2, :].rearrange("p x (m w) -> p w x m", w=WW)
            dst = big[:, q % 2, :].rearrange("p (c y w) -> p y w c", c=CH, y=2)[:, y]
            return nc.vector.transpose(dst, src)

        def mover_program(engine, eng):
            eng.wait_ge(const_in, CONSTS)
            with eng.Fori(0, GROUPS) as g:
                for k, (stage, q, i) in enumerate(LIFT.steps):
                    if LIFT.by[k] == engine:
                        eng.wait_ge(filled, g * GROUP_FILLED + (k + 1))
                        move(engine, k, stage, q, i).then_inc(moved[engine], 1)
                if engine == "dve":
                    for e in moved:
                        eng.wait_ge(moved[e], g * GROUP_MOVED[e] + LIFT.moved[e])
                    for y in range(2):
                        turn(0, y).then_inc(turned, 1)
                with eng.Fori(0, LAYERS) as l:
                    start = g * GROUP_FILLED + l * LAYER.count
                    at = {e: g * GROUP_MOVED[e] + l * LAYER.moved[e] for e in moved}
                    if engine == "dve":
                        eng.wait_ge(moved["act"], at["act"] + LIFT.moved["act"])
                        for y in range(2):
                            turn(1, y).then_inc(turned, 1)
                        nc.vector.tensor_copy(conv_b[:, :], conv_b_all[:, bass.ds(l, 1)]).then_inc(conv_w_set, 1)
                        nc.vector.tensor_copy(conv_w[:, :], conv_all[:, bass.ds(l, 1), :].rearrange(
                            "p a n -> p (a n)")).then_inc(conv_w_set, 1)
                    for k, (stage, q, i) in enumerate(LAYER.steps):
                        if engine == "dve" and stage == "fwd_rows" and q < QUADS - 2 and i == 3:
                            eng.wait_ge(filled, start + (LIFT.count + k + 1))
                            for y in range(2):
                                turn(q + 2, y).then_inc(turned, 1)
                        if LAYER.by[k] == engine:
                            if (stage, q, i) == ("out", 0, 0):
                                eng.wait_ge(conv_w_set, g * (2 * LAYERS) + (l * 2 + 2))
                            eng.wait_ge(filled, start + (LIFT.count + k + 1))
                            move(engine, k, stage, q, i, l).then_inc(moved[engine], 1)
                    if engine == "dve":
                        _, n = LAYER.moved_at(LAYER.index["out", 0, QB - 1])
                        eng.wait_ge(moved["act"], at["act"] + (LIFT.moved["act"] + n))
                        eng.wait_ge(filled, start + (LIFT.count + LAYER.index["out", 2, QB - 1] + 1))
                        for y in range(2):
                            turn(0, y).then_inc(turned, 1)
                start = LIFT.count + LAYERS * LAYER.count
                for k, (stage, q, i) in enumerate(HEAD.steps):
                    if HEAD.by[k] == engine:
                        if stage == "fc2" and q >= 2:
                            eng.wait_ge(h_out[q % 2], g * (8 * GB) + 32 * (q // 2))
                        eng.wait_ge(filled, g * GROUP_FILLED + (start + k + 1))
                        move(engine, k, stage, q, i).then_inc(moved[engine], 1)
                if engine == "dve":
                    for b in range(2):
                        eng.wait_ge(h_out[b], g * (8 * GB) + 8 * GB)

        @block.vector
        def _(dve):
            nc.vector.memset(lift_w[:], 0.0)
            nc.vector.memset(conv_all[:], 0.0)
            nc.vector.memset(w1[:], 0.0)
            nc.vector.memset(w2[:], 0.0)
            nc.vector.memset(modes_t[:], 0.0)
            nc.vector.memset(slots[:], 0.0)
            dve.drain().then_inc(zeroed, 1)
            mover_program("dve", dve)

        @block.scalar
        def _(act):
            mover_program("act", act)


def centre(nc, link, src, centred, squares, stats):
    link(nc.vector.tensor_reduce(stats[:, 0, :], src, AX_X, ALU.add))
    link(nc.vector.tensor_scalar(stats[:, 1, :], stats[:, 0, :], -1.0 / D, None, ALU.mult))
    link(nc.vector.tensor_tensor(centred, src, along(stats[:, 1, :], D), ALU.add))
    link(nc.vector.tensor_tensor(squares, centred, centred, ALU.mult))
    link(nc.vector.tensor_reduce(stats[:, 0, :], squares, AX_X, ALU.add))
    return nc.vector.tensor_scalar(stats[:, 1, :], stats[:, 0, :], 1.0 / D, EPS, ALU.mult, ALU.add)


def root(nc, stats):
    return nc.scalar.activation(stats[:, 2, :], stats[:, 1, :], ACT.Sqrt)


def invert_root(nc, link, stats):
    link(nc.vector.reciprocal(stats[:, 0, :], stats[:, 2, :]))
    link(nc.vector.tensor_tensor(stats[:, 0, :], stats[:, 0, :], stats[:, 1, :], ALU.mult))
    link(nc.vector.tensor_tensor(stats[:, 0, :], stats[:, 0, :], stats[:, 2, :], ALU.add))
    link(nc.vector.tensor_scalar(stats[:, 1, :], stats[:, 0, :], 0.5, None, ALU.mult))
    link(nc.vector.reciprocal(stats[:, 2, :], stats[:, 1, :]))


ATTENTION = Steps([("x_turn", 0, c) for c in range(4)] + [("qkv", 0, c) for c in range(8)]
                  + [("qk_turn", k, c) for c in range(4) for k in range(2)]
                  + [("scores", 0, c) for c in range(4)] + [("attend", 0, c) for c in range(2)])
ROUTING = Steps([("y_turn", 0, c) for c in range(4)] + [("gate", 0, c) for c in range(4)]
                + [("s_turn", 0, c) for c in range(4)])


def attention(nc, slots, ident, h2, h_dram, wqkv, k_rope, k_decay):
    with ExitStack() as ctx:
        def sb(name, shape, dt=F32):
            return ctx.enter_context(nc.sbuf_tensor(name, shape, dt))

        def sem(name):
            return ctx.enter_context(nc.semaphore(name))

        h = sb("at_h", [128, TILES, D])
        centred = sb("at_centred", [128, TILES, D])
        squares = sb("at_squares", [128, TILES, D])
        normed = sb("at_normed", [128, TILES, D])
        stats = sb("at_stats", [128, 3, TILES])
        w = sb("at_w", [D, 3 * D])
        rope = sb("at_rope", [128, 4, D])
        decay = sb("at_decay", [128, 128])
        normed_t = sb("at_normed_t", [D, TOKENS])
        qkv = sb("at_qkv", [128, TILES, 3 * D])
        turned = sb("at_turned", [128, 2, TILES, D])
        qk_t = sb("at_qk_t", [D, 2, TOKENS])
        ret_t = sb("at_ret_t", [128, TILES, 128])

        h_in = sem("at_h_in")
        weights_in = sem("at_weights_in")
        chain = sem("at_chain")
        norm_done = sem("at_norm_done")
        variance_done = sem("at_variance_done")
        root_done = sem("at_root_done")
        rope_done = sem("at_rope_done")
        filled = sem("at_filled")
        moved = {"dve": sem("at_moved_dve"), "act": sem("at_moved_act")}
        block = ctx.enter_context(nc.Block())

        @block.sync
        def _(sp):
            src = h_dram.rearrange("(q a) (y x) (r s w) -> x s a y r q w", a=4, x=2, s=2, w=WW)
            dst = h[:].rearrange("p (q y) w -> p y q w", y=2)
            for x in range(2):
                for s in range(2):
                    for a in range(4):
                        at = x * HH + s * HALF + a * 8
                        for y in range(2):
                            sp.dma_start(dst[at:at + 8, y], src[x, s, a, y]).then_inc(h_in, 16)
            sp.dma_start(w[:], wqkv).then_inc(weights_in, 16)
            sp.dma_start(flat(rope[:]), k_rope).then_inc(weights_in, 16)
            sp.dma_start(decay[:], k_decay).then_inc(weights_in, 16)

        @block.tensor
        def _(pe):
            pe.wait_ge(weights_in, 48)
            for k, (stage, q, i) in enumerate(ATTENTION.steps):
                s = slots[:, k % SLOTS, :]
                if k >= SLOTS:
                    e, n = ATTENTION.moved_at(k - SLOTS)
                    pe.wait_ge(moved[e], n)
                if (stage, i) == ("x_turn", 0):
                    pe.wait_ge(norm_done, 1)
                if (stage, i) == ("qkv", 0):
                    for e, n in ATTENTION.outputs_of("x_turn", 0):
                        pe.wait_ge(moved[e], n)
                if (stage, i) == ("qk_turn", 0):
                    pe.wait_ge(rope_done, q + 1)
                if (stage, i) == ("scores", 0):
                    for part in range(2):
                        for e, n in ATTENTION.outputs_of("qk_turn", part):
                            pe.wait_ge(moved[e], n)
                if (stage, i) == ("attend", 0):
                    for e, n in ATTENTION.outputs_of("scores", 0):
                        pe.wait_ge(moved[e], n)
                if stage == "x_turn":
                    for j in range(8):
                        mm = nc.tensor.transpose(s[0:D, j * 128:(j + 1) * 128],
                                                 normed[:, 8 * i + j, :], ident[:, :])
                elif stage == "qkv":
                    for j in range(4):
                        at = (4 * i + j) * 128
                        mm = nc.tensor.matmul(s[:, j * 256:j * 256 + 3 * D], normed_t[:, at:at + 128],
                                              w[:, :], start=True, stop=True)
                elif stage == "qk_turn":
                    for j in range(8):
                        mm = nc.tensor.transpose(s[0:D, j * 128:(j + 1) * 128],
                                                 turned[:, q, 8 * i + j, :], ident[:, :])
                elif stage == "scores":
                    for j in range(8):
                        at = (8 * i + j) * 128
                        mm = nc.tensor.matmul(s[:, j * 128:(j + 1) * 128], qk_t[:, 1, at:at + 128],
                                              qk_t[:, 0, at:at + 128], start=True, stop=True)
                else:
                    for j in range(16):
                        t = 16 * i + j
                        mm = nc.tensor.matmul(s[:, j * D:(j + 1) * D], ret_t[:, t, :],
                                              qkv[:, t, 2 * D:3 * D], start=True, stop=True)
                mm.then_inc(filled, 1)

        def mover_program(engine, eng):
            for k, (stage, q, i) in enumerate(ATTENTION.steps):
                if ATTENTION.by[k] != engine:
                    continue
                s = slots[:, k % SLOTS, :]
                if engine == "dve" and (stage, q, i) == ("qk_turn", 0, 0):
                    rotate(eng)
                eng.wait_ge(filled, k + 1)
                if stage == "x_turn":
                    dst, src = normed_t[:, i * SLOT:(i + 1) * SLOT], s[0:D, :]
                elif stage == "qkv":
                    dst = qkv[:, 4 * i:4 * i + 4, :]
                    src = s.rearrange("p (t n) -> p t n", t=4)[:, :, 0:3 * D]
                elif stage == "qk_turn":
                    dst, src = qk_t[:, q, i * SLOT:(i + 1) * SLOT], s[0:D, :]
                if stage == "scores":
                    ins = nc.vector.tensor_tensor(ret_t[:, 8 * i:8 * i + 8, :],
                                                  s.rearrange("p (t n) -> p t n", t=8),
                                                  across(decay[:, :], 8), ALU.mult)
                elif stage == "attend":
                    ins = nc.vector.tensor_tensor(h2[:, 16 * i:16 * i + 16, :],
                                                  s.rearrange("p (t n) -> p t n", n=D),
                                                  h[:, 16 * i:16 * i + 16, :], ALU.add)
                elif engine == "dve":
                    ins = nc.vector.tensor_copy(dst, src)
                else:
                    ins = nc.scalar.copy(dst, src)
                ins.then_inc(moved[engine], 1)

        steps = [0]

        def rotate(dve):
            for e, n in ATTENTION.outputs_of("qkv", 0):
                dve.wait_ge(moved[e], n)
            for k in range(2):
                src = qkv[:, :, k * D:(k + 1) * D]
                cos, sin = rope[:, 2 * k, :], rope[:, 2 * k + 1, :]
                nc.vector.tensor_tensor(centred[:], src, across(cos, TILES), ALU.mult)
                swapped = squares[:].rearrange("p t (i r) -> p t i r", r=2)
                pairs = src.rearrange("p t (i r) -> p t i r", r=2)
                for r in range(2):
                    table = sin.rearrange("p (i r) -> p i r", r=2)[:, :, r]
                    steps[0] += 1
                    nc.vector.tensor_tensor(swapped[:, :, :, r], pairs[:, :, :, 1 - r],
                                            across(table, TILES), ALU.mult).then_inc(chain, 1)
                dve.wait_ge(chain, steps[0])
                nc.vector.tensor_tensor(turned[:, k, :, :], centred[:], squares[:],
                                        ALU.add).then_inc(rope_done, 1)
                dve.wait_ge(rope_done, k + 1)

        @block.vector
        def _(dve):
            def link(ins):
                steps[0] += 1
                ins.then_inc(chain, 1)
                dve.wait_ge(chain, steps[0])

            dve.wait_ge(h_in, 16 * 32)
            dve.wait_ge(weights_in, 48)
            centre(nc, link, h[:], centred[:], squares[:], stats).then_inc(variance_done, 1)
            dve.wait_ge(root_done, 1)
            invert_root(nc, link, stats)
            nc.vector.tensor_tensor(normed[:], centred[:], along(stats[:, 2, :], D),
                                    ALU.mult).then_inc(norm_done, 1)
            dve.wait_ge(norm_done, 1)
            mover_program("dve", dve)

        @block.scalar
        def _(act):
            act.wait_ge(variance_done, 1)
            root(nc, stats).then_inc(root_done, 1)
            mover_program("act", act)


def experts(nc, slots, ident, h2, gate_t, lattice, out_wt, out_b, ln_g, ln_b, k_select, out):
    with ExitStack() as ctx:
        def sb(name, shape, dt=F32):
            return ctx.enter_context(nc.sbuf_tensor(name, shape, dt))

        def sem(name):
            return ctx.enter_context(nc.semaphore(name))

        EB = EXPERTS // 2
        PB = 3
        y2 = sb("ex_y2", [128, TILES, 2, D])
        centred = sb("ex_centred", [128, TILES, D])
        squares = sb("ex_squares", [128, TILES, D])
        stats = sb("ex_stats", [128, 3, TILES])
        gate_w = sb("ex_gate_w", [128, PAD_N])
        lattice_w = sb("ex_lattice_w", [128, EB, D])
        out_w = sb("ex_out_w", [128, D])
        vectors = sb("ex_vectors", [128, 3, D])
        y_t = sb("ex_y_t", [128, TOKENS])
        logits = sb("ex_logits", [128, TILES, EXPERTS])
        top = sb("ex_top", [128, TILES, 8])
        above = sb("ex_above", [128, TILES, EXPERTS])
        level = sb("ex_level", [128, TILES, EXPERTS])
        run = sb("ex_run", [128, 2, TILES, EXPERTS])
        halves = sb("ex_halves", [128, TILES, 2, EXPERTS])
        halves_t = sb("ex_halves_t", [128, TOKENS], F32R)
        select = sb("ex_select", [128, EB * 128], F32R)
        weighted = sb("ex_weighted", [128, PB, SLOT])
        mixed = sb("ex_mixed", [128, 4, 512])

        weights_in = sem("ex_weights_in")
        zeroed = sem("ex_zeroed")
        chain = sem("ex_chain")
        norm_done = sem("ex_norm_done")
        variance_done = sem("ex_variance_done")
        root_done = sem("ex_root_done")
        copied = sem("ex_copied")
        shifted = sem("ex_shifted")
        exp_done = sem("ex_exp_done")
        halves_done = sem("ex_halves_done")
        filled = sem("ex_filled")
        moved = {"dve": sem("ex_moved_dve"), "act": sem("ex_moved_act")}
        spread = sem("ex_spread")
        weigh = sem("ex_weigh")
        summed = sem("ex_summed")
        mixed_out = sem("ex_mixed_out")
        projected = sem("ex_projected")
        result = sem("ex_result")
        stored = sem("ex_stored")
        block = ctx.enter_context(nc.Block())
        select_raw = y2[:].rearrange("p t a d -> p (t a d)")

        @block.sync
        def _(sp):
            sp.dma_start(select_raw, k_select).then_inc(weights_in, 16)
            sp.dma_start(flat(lattice_w[:]), lattice).then_inc(weights_in, 16)
            for half in range(2):
                sp.dma_start(out_w[half * D:(half + 1) * D, :], out_wt).then_inc(weights_in, 16)
            for n, v in enumerate((out_b, ln_g, ln_b)):
                sp.dma_start(vectors[:, n, :], v.rearrange("(a d) -> a d", a=1).broadcast_to(
                    [128, D])).then_inc(weights_in, 16)
            sp.wait_ge(zeroed, 1)
            sp.dma_start(gate_w[0:D, 0:EXPERTS], gate_t).then_inc(weights_in, 16)
            sp.wait_ge(result, 1)
            sp.dma_start(out.rearrange("(t b) h w -> (b h) t w", b=2), squares[:]).then_inc(stored, 16)
            sp.wait_ge(stored, 16)

        @block.tensor
        def _(pe):
            pe.wait_ge(weights_in, 128)
            for k, (stage, q, i) in enumerate(ROUTING.steps):
                s = slots[:, k % SLOTS, :]
                if k >= SLOTS:
                    e, n = ROUTING.moved_at(k - SLOTS)
                    pe.wait_ge(moved[e], n)
                if (stage, i) == ("y_turn", 0):
                    pe.wait_ge(norm_done, 1)
                    pe.wait_ge(copied, 1)
                if (stage, i) == ("gate", 0):
                    for e, n in ROUTING.outputs_of("y_turn", 0):
                        pe.wait_ge(moved[e], n)
                if (stage, i) == ("s_turn", 0):
                    pe.wait_ge(halves_done, 1)
                for j in range(8):
                    t = 8 * i + j
                    if stage == "gate":
                        mm = nc.tensor.matmul(s[:, j * 128:j * 128 + PAD_N], y_t[:, t * 128:(t + 1) * 128],
                                              gate_w[:, :], start=True, stop=True)
                    else:
                        src = y2 if stage == "y_turn" else halves
                        mm = nc.tensor.transpose(s[:, j * 128:(j + 1) * 128], flat(src[:, t, :, :]),
                                                 ident[:, :])
                mm.then_inc(filled, 1)
            for e in moved:
                pe.wait_ge(moved[e], ROUTING.moved[e])
            with pe.Fori(0, 4) as g:
                def spread_block(n):
                    if n >= PB:
                        pe.wait_ge(weigh, g * EB + (n - PB + 1))
                    for j in range(2):
                        mm = nc.tensor.matmul(slots[:, n % PB, j * 512:(j + 1) * 512],
                                              select[:, n * 128:(n + 1) * 128],
                                              halves_t[:, bass.ds(g * SLOT + j * 512, 512)],
                                              start=True, stop=True)
                    mm.then_inc(spread, 1)

                for n in range(PB - 1):
                    spread_block(n)
                for n in range(EB):
                    if n + PB - 1 < EB:
                        spread_block(n + PB - 1)
                    pe.wait_ge(weigh, g * EB + (n + 1))
                    for j in range(2):
                        mm = nc.tensor.matmul(slots[j * D:(j + 1) * D, SLOTS - 1, 0:512],
                                              lattice_w[:, n, :], weighted[:, n % PB, j * 512:(j + 1) * 512],
                                              start=(n == 0), stop=(n == EB - 1))
                mm.then_inc(summed, 1)
                pe.wait_ge(mixed_out, g + 1)
            for i in range(2):
                for j in range(16):
                    t = 16 * i + j
                    half = t % 8 // 4
                    rows = slice(half * D, half * D + D)
                    at = t % 4 * 128
                    to = half * 512 + (j // 8 * 4 + t % 4) * D
                    mm = nc.tensor.matmul(slots[:, i, to:to + D], mixed[rows, t // 8, at:at + 128],
                                          out_w[rows, :], start=True, stop=True)
                mm.then_inc(projected, 1)

        def mover_program(engine, eng):
            for k, (stage, q, i) in enumerate(ROUTING.steps):
                if engine == "dve" and (stage, i) == ("s_turn", 0):
                    route(eng)
                if engine == "act" and (stage, i) == ("s_turn", 0):
                    eng.wait_ge(shifted, 1)
                    nc.scalar.activation(level[:], level[:], ACT.Exp).then_inc(exp_done, 1)
                if ROUTING.by[k] != engine:
                    continue
                s = slots[:, k % SLOTS, :]
                eng.wait_ge(filled, k + 1)
                if stage == "gate":
                    dst = logits[:, 8 * i:8 * i + 8, :]
                    src = s.rearrange("p (t n) -> p t n", t=8)[:, :, 0:EXPERTS]
                else:
                    dst = (y_t if stage == "y_turn" else halves_t)[:, i * SLOT:(i + 1) * SLOT]
                    src = s
                if engine == "dve":
                    nc.vector.tensor_copy(dst, src).then_inc(moved[engine], 1)
                else:
                    nc.scalar.copy(dst, src).then_inc(moved[engine], 1)

        steps = [0]

        def linked(dve):
            def link(ins):
                steps[0] += 1
                ins.then_inc(chain, 1)
                dve.wait_ge(chain, steps[0])
            return link

        def route(dve):
            link = linked(dve)
            for e, n in ROUTING.outputs_of("gate", 0):
                dve.wait_ge(moved[e], n)
            for t in range(TILES):
                last = nc.vector.max(top[:, t, :], logits[:, t, :])
            link(last)
            least, most = top[:, :, TOP_K - 1], top[:, :, 0]
            nc.vector.tensor_tensor(level[:], logits[:], along(most, EXPERTS),
                                    ALU.subtract).then_inc(shifted, 1)
            nc.vector.tensor_tensor(run[:, 0], logits[:], along(least, EXPERTS), ALU.is_equal)
            link(nc.vector.tensor_tensor(above[:], logits[:], along(least, EXPERTS), ALU.is_gt))
            nc.vector.tensor_copy(squares[:], run[:, 0])
            link(nc.vector.tensor_reduce(stats[:, 0, :], above[:], AX_X, ALU.add))
            link(nc.vector.tensor_scalar(stats[:, 1, :], stats[:, 0, :], -1.0, float(TOP_K),
                                         ALU.mult, ALU.add))
            shift, at = 1, 0
            while shift < EXPERTS:
                nc.vector.tensor_copy(run[:, 1 - at, :, 0:shift], run[:, at, :, 0:shift])
                link(nc.vector.tensor_tensor(run[:, 1 - at, :, shift:], run[:, at, :, shift:],
                                             run[:, at, :, 0:EXPERTS - shift], ALU.add))
                shift, at = 2 * shift, 1 - at
            link(nc.vector.tensor_tensor(run[:, 1 - at], run[:, at], along(stats[:, 1, :], EXPERTS),
                                         ALU.is_le))
            link(nc.vector.tensor_tensor(run[:, at], run[:, 1 - at], squares[:], ALU.mult))
            link(nc.vector.tensor_tensor(above[:], above[:], run[:, at], ALU.add))
            dve.wait_ge(exp_done, 1)
            link(nc.vector.tensor_tensor(squares[:], level[:], above[:], ALU.mult))
            link(nc.vector.tensor_reduce(stats[:, 0, :], squares[:], AX_X, ALU.add))
            link(nc.vector.reciprocal(stats[:, 1, :], stats[:, 0, :]))
            link(nc.vector.tensor_tensor(level[:], squares[:], along(stats[:, 1, :], EXPERTS), ALU.mult))
            link(nc.vector.tensor_copy(halves[:, :, 0, :].bitcast(F32R), level[:]))
            nc.vector.tensor_tensor(halves[:, :, 1, :], level[:], halves[:, :, 0, :],
                                    ALU.subtract).then_inc(halves_done, 1)

        @block.vector
        def _(dve):
            link = linked(dve)
            nc.vector.memset(gate_w[:], 0.0).then_inc(zeroed, 1)
            dve.wait_ge(weights_in, 128)
            link(nc.vector.tensor_copy(select[:], select_raw))
            centre(nc, link, h2[:], centred[:], squares[:], stats).then_inc(variance_done, 1)
            dve.wait_ge(root_done, 1)
            invert_root(nc, link, stats)
            nc.vector.tensor_tensor(y2[:, :, 0, :], centred[:], along(stats[:, 2, :], D),
                                    ALU.mult).then_inc(norm_done, 1)
            mover_program("dve", dve)
            for e in moved:
                dve.wait_ge(moved[e], ROUTING.moved[e])
            with dve.Fori(0, 4) as g:
                for n in range(EB):
                    dve.wait_ge(spread, g * EB + (n + 1))
                    nc.vector.tensor_tensor(weighted[:, n % PB, :], slots[:, n % PB, :],
                                            y_t[:, bass.ds(g * SLOT, SLOT)], ALU.mult).then_inc(weigh, 1)
            nc.vector.tensor_tensor(level[:], y2[:, :, 0, :], across(vectors[:, 0, :], TILES),
                                    ALU.add).then_inc(chain, 1)
            steps[0] += 1
            dve.wait_ge(chain, steps[0])
            for i in range(2):
                dve.wait_ge(projected, i + 1)
                part = level[:, 16 * i:16 * i + 16, :].rearrange("p (a h t) d -> p a h (t d)", a=2, h=2)
                link(nc.vector.tensor_tensor(
                    part, slots[:, i, :].rearrange("p (h a n) -> p a h n", a=2, h=2), part, ALU.add))
            centre(nc, link, level[:], centred[:], squares[:], stats).then_inc(variance_done, 1)
            dve.wait_ge(root_done, 2)
            invert_root(nc, link, stats)
            link(nc.vector.tensor_tensor(level[:], centred[:], along(stats[:, 2, :], D), ALU.mult))
            link(nc.vector.tensor_tensor(level[:], level[:], across(vectors[:, 1, :], TILES), ALU.mult))
            link(nc.vector.tensor_tensor(centred[:], h2[:], across(vectors[:, 2, :], TILES), ALU.add))
            nc.vector.tensor_tensor(squares[:], level[:], centred[:], ALU.add).then_inc(result, 1)

        @block.scalar
        def _(act):
            act.wait_ge(variance_done, 1)
            root(nc, stats).then_inc(root_done, 1)
            act.wait_ge(norm_done, 1)
            nc.scalar.copy(y2[:, :, 1, :], y2[:, :, 0, :]).then_inc(copied, 1)
            mover_program("act", act)
            with act.Fori(0, 4) as g:
                act.wait_ge(summed, g + 1)
                nc.scalar.copy(mixed[:, bass.ds(g, 1), :].rearrange("p a n -> p (a n)"),
                               slots[:, SLOTS - 1, 0:512]).then_inc(mixed_out, 1)
            act.wait_ge(variance_done, 2)
            root(nc, stats).then_inc(root_done, 1)


def build(nc, x, fc0_w, fc0_b, sw, cwt, cb, fc1_w, fc1_b, fc2_w, fc2_b, wqkv, gate_t, lattice,
          out_wt, out_b, ln_g, ln_b, k_fwd_rows, k_fwd_cols, k_inv_rows, k_inv_cols, k_rope, k_decay, k_select,
          k_ident, out):
    h_dram = nc.dram_tensor("h_scratch", (IMAGES // QB * 4, QB, PART), F32, kind="Internal").ap()
    with (
        nc.psum_tensor("slots", [128, SLOTS, SLOT], F32) as slots,
        nc.sbuf_tensor("ident", [128, 128], F32) as ident,
        nc.semaphore("ident_in") as ident_in,
    ):
        nc.sync.dma_start(ident[:, :], k_ident).then_inc(ident_in, 16)
        tower(nc, slots, ident, ident_in, h_dram, x, fc0_w, fc0_b, sw, cwt, cb, fc1_w, fc1_b, fc2_w,
              fc2_b, k_fwd_rows, k_fwd_cols, k_inv_rows, k_inv_cols)
        with nc.sbuf_tensor("h2", [128, TILES, D], F32) as h2:
            attention(nc, slots, ident, h2, h_dram, wqkv, k_rope, k_decay)
            experts(nc, slots, ident, h2, gate_t, lattice, out_wt, out_b, ln_g, ln_b, k_select, out)


def kernel(**inputs):
    import numpy as _np
    import concourse.bacc as _bacc
    from concourse import mybir as _mybir
    from concourse.bass_utils import run_bass_kernel_spmd as _run

    f = {n: _np.asarray(a) for n, a in inputs.items()}
    t = "L0_tok_"
    order = [(n + 1) % LAYERS for n in range(LAYERS)]
    sw = [f[f"{t}sw{n}"].transpose(3, 0, 2, 1) for n in order]
    sw = _np.stack(sw).reshape(LAYERS, BLOCKS, 4, CH, MODES, CH).transpose(0, 2, 3, 1, 4, 5)
    wq, wk = f["L0_attn_W_Q"], f["L0_attn_W_K"]
    fwd_rows, fwd_cols, inv_rows, inv_cols = dft_constants()
    rope, decay, select = attention_constants()
    arrays = {
        "x": f["x"].reshape(GROUPS, GB, 2, 4, 8, WW, 3).transpose(0, 1, 3, 6, 4, 2, 5).reshape(
            GROUPS, GB * 12, PART),
        "fc0_w": f[t + "fc0_w"], "fc0_b": f[t + "fc0_b"],
        "sw": sw.reshape(LAYERS, 128, BLOCKS * MODES * CH),
        "cwt": _np.stack([f[f"{t}cw{n}"].T for n in range(LAYERS)]),
        "cb": _np.stack([f[f"{t}cb{n}"] for n in range(LAYERS)], axis=1),
        "fc1_w": f[t + "fc1_w"], "fc1_b": f[t + "fc1_b"],
        "fc2_w": f[t + "fc2_w"], "fc2_b": f[t + "fc2_b"],
        "wqkv": _np.concatenate([wq, wk, f["L0_attn_W_V"]], axis=1),
        "gate_t": f["L0_ffn_gate_w"].T,
        "lattice": f["L0_ffn_lattice_weights"].reshape(EXPERTS // 2, 2, D, D).transpose(1, 2, 0, 3).reshape(128, -1),
        "out_wt": f["L0_ffn_out_w"].T, "out_b": f["L0_ffn_out_b"],
        "ln_g": f["L0_ffn_ln_g"], "ln_b": f["L0_ffn_ln_b"],
        "k_fwd_rows": fwd_rows, "k_fwd_cols": fwd_cols,
        "k_inv_rows": inv_rows, "k_inv_cols": inv_cols,
        "k_rope": rope, "k_decay": decay, "k_select": select,
        "k_ident": _np.eye(128, dtype=_np.float32),
    }
    nc = _bacc.Bacc("TRN2", target_bir_lowering=False, num_devices=1)
    arrays = {f"in_{n}_dram": _np.ascontiguousarray(a) for n, a in arrays.items()}
    args = [nc.dram_tensor(n, a.shape, _mybir.dt.from_np(a.dtype), kind="ExternalInput").ap()
            for n, a in arrays.items()]
    out = nc.dram_tensor("out_0_dram", (IMAGES, HH, WW), _mybir.dt.float32, kind="ExternalOutput").ap()
    build(nc, *args, out)
    r = _run(nc, [arrays], core_ids=[0])
    return r.results[0]["out_0_dram"]
```

```python
from contextlib import ExitStack

import numpy as np

import concourse.bass as bass
from concourse import mybir

F32 = mybir.dt.float32
F32R = mybir.dt.float32r
ALU = mybir.AluOpType
ACT = mybir.ActivationFunctionType
AX_X = mybir.AxisListType.X

IMAGES, HH, WW = 64, 64, 64
CH = 32
MODES = 20
LAYERS = 4
QB = 4
GB = 16
QUADS = GB // QB
GROUPS = IMAGES // GB
HALF = HH // 2
SPATIAL = HH * WW
PART = SPATIAL // 4
PAD_N = 96
PAD_K = 96
BLOCKS = MODES // 4
HID = 64
IN_CH = 4
LIFT_E = 32 // IN_CH
LIFT_T = 2 * QUADS * MODES // LIFT_E
SLOT = 1024
SLOTS = 4
TOKENS = IMAGES * HH
TILES = TOKENS // 128
D = 64
EXPERTS = 64
TOP_K = 6
EPS = 1e-5


def dft_constants():
    k = np.arange(MODES)
    norm = 1.0 / np.sqrt(HH * WW)
    pos = np.arange(HH)
    angle = 2 * np.pi * np.outer(pos, k) / HH
    cos, sin = np.cos(angle), np.sin(angle)
    twice = np.where(k == 0, 1.0, 2.0)
    rows_fwd = np.zeros((128, PAD_N))
    cols_fwd = np.zeros((2, WW, 2, 4, 8, 2, 2))
    for part in range(128):
        a, x, r, s = part // 32, part // 16 % 2, part // 2 % 8, part % 2
        h = 32 * s + 8 * a + r
        rows_fwd[part, x * 40:x * 40 + 40:2] = norm * cos[h]
        rows_fwd[part, x * 40 + 1:x * 40 + 40:2] = -norm * sin[h]
    for y in range(2):
        for kw in range(MODES):
            m, j = kw // 4, kw % 4
            cols_fwd[y, :, 0, j, m, y, 0] = twice[kw] * cos[:, kw]
            cols_fwd[y, :, 0, j, m, y, 1] = -twice[kw] * sin[:, kw]
            cols_fwd[y, :, 1, j, m, y, 0] = twice[kw] * sin[:, kw]
            cols_fwd[y, :, 1, j, m, y, 1] = twice[kw] * cos[:, kw]
    rows_inv = np.zeros((PAD_K, 2, 2, 2, HALF))
    for y in range(2):
        for kh in range(MODES):
            at, p = 4 * kh + 2 * y, kh % 2
            rows_inv[at, y, p, 0] = cos[:HALF, kh]
            rows_inv[at + 1, y, p, 0] = -sin[:HALF, kh]
            rows_inv[at, y, p, 1] = sin[:HALF, kh]
            rows_inv[at + 1, y, p, 1] = cos[:HALF, kh]
    places = np.concatenate([np.arange(MODES // 2), 16 + np.arange(MODES // 2)])
    cols_inv = np.zeros((2, 2, 32, 2, WW))
    for p in range(2):
        for s in range(2):
            sign = -1.0 if s * p else 1.0
            cols_inv[p, 0, places, s] = sign * norm * cos.T
            cols_inv[p, 1, places, s] = -sign * norm * sin.T
    f32 = np.float32
    return (rows_fwd.astype(f32), cols_fwd.reshape(128, -1).astype(f32),
            rows_inv.reshape(PAD_K, -1).astype(f32), cols_inv.reshape(128, -1).astype(f32))


def lift_mask():
    mask = np.zeros((4, LIFT_E, IN_CH, LIFT_E, 4), np.float32)
    for j in range(4):
        for e in range(LIFT_E):
            mask[j, e, :, e, j] = 1.0
    return mask.reshape(128, -1)


def attention_constants():
    f = np.float32
    gamma, scale_base = 0.96875, 512.0
    even = np.arange(0, D, 2, dtype=f)
    inv_freq = (f(1.0) / f(10000.0) ** (even / f(D))).astype(f)
    pos = np.arange(HH, dtype=f)
    ang = pos[:, None] * inv_freq[None, :]
    sin, cos = np.sin(ang), np.cos(ang)
    base = (even + f(0.4 * D)) / f(1.4 * D)
    scale = base[None, :] ** (pos[:, None] / f(scale_base))
    rope = np.zeros((128, 4, D), f)
    for k, sc in enumerate((scale, 1.0 / scale)):
        for image in range(2):
            rows = slice(image * HH, image * HH + HH)
            rope[rows, 2 * k, 0::2] = cos * sc
            rope[rows, 2 * k, 1::2] = cos * sc
            rope[rows, 2 * k + 1, 0::2] = -sin * sc
            rope[rows, 2 * k + 1, 1::2] = sin * sc
    decay = np.zeros((128, 128), f)
    for image in range(2):
        for m in range(HH):
            n = np.arange(m, HH)
            decay[image * HH + m, image * HH + n] = gamma ** (n - m)
    select = np.zeros((2, EXPERTS, EXPERTS // 2, 2, D), f)
    for e in range(EXPERTS):
        select[:, e, e // 2, e % 2, :] = 1.0
    return rope.reshape(128, -1), decay, select.reshape(128, -1)


def back_steps():
    s = [("mix", 0, i) for i in range(BLOCKS)]
    s += [("modes_turn", 0, 0), ("modes_turn", 0, 1), ("modes_turn", 1, 0)]
    s += [("inv_rows", 0, i) for i in range(4)]
    s += [("modes_turn", 1, 1)]
    for q in range(QUADS):
        for i in range(4):
            s.append(("out", q, i))
            if q + 1 < QUADS:
                s.append(("inv_rows", q + 1, i))
            if q + 2 < QUADS and i % 2:
                s.append(("modes_turn", q + 2, i // 2))
    return s


def first_layer_steps():
    return [("lift", 0, i) for i in range(LIFT_E // 2)] + back_steps()


COLS_PARTS = [(0, 0, MODES), (1, 0, MODES), (0, 0, MODES // 2), (0, MODES // 2, MODES),
              (1, 0, MODES // 2), (1, MODES // 2, MODES)]


def layer_steps():
    s = []
    for q in range(QUADS):
        for i in range(4):
            s.append(("fwd_rows", q, i))
            if i == 1 and q > 0:
                s += [("fwd_cols", q - 1, j) for j in ((0, 1) if q < QUADS - 1 else (0,))]
    s += [("fwd_cols", QUADS - 2, 4), ("fwd_cols", QUADS - 2, 5)]
    return s + [("fwd_cols", QUADS - 1, j) for j in range(2, 6)] + back_steps()


def mover(stage, q, i):
    if stage in ("out", "fc1"):
        return "act"
    if stage == "in_rows":
        return "act" if q % 2 else "dve"
    if stage in ("fwd_rows", "lift", "mix", "x_turn", "qkv", "y_turn", "gate", "s_turn"):
        return "act" if i % 2 else "dve"
    if stage == "qk_turn":
        return "act" if q else "dve"
    return "dve"


class Steps:

    def __init__(self, steps):
        self.first_slot = -len(steps) % SLOTS
        self.steps = steps
        self.index = {s: k for k, s in enumerate(steps)}
        self.by = [mover(*s) for s in steps]
        self.count = len(steps)
        self.moved = {e: sum(b == e for b in self.by) for e in ("dve", "act")}

    def moved_at(self, k):
        return self.by[k], sum(b == self.by[k] for b in self.by[:k + 1])

    def outputs_of(self, stage, q):
        last = {}
        for k, (st, qq, _) in enumerate(self.steps):
            if (st, qq) == (stage, q):
                e, n = self.moved_at(k)
                last[e] = n
        return last.items()


EARLY_STEPS = [("in_rows", q, 0) for q in range(QUADS)] + [("in_cols", 0, i) for i in range(4)]


def head_steps():
    s = []
    for q in range(QUADS):
        for i in range(4):
            s += [("fc1", 2 * q, i), ("fc1", 2 * q + 1, i)]
            if i == 0 and q > 0:
                s += [("fc2", 2 * q - 2, 0), ("fc2", 2 * q - 1, 0)]
    s += EARLY_STEPS[:QUADS] + [("fc2", 2 * QUADS - 2, 0), ("fc2", 2 * QUADS - 1, 0)]
    return s + EARLY_STEPS[QUADS:]


FIRST = Steps(first_layer_steps())
LAYER = Steps(layer_steps())
HEAD = Steps(head_steps())
EARLY = Steps(EARLY_STEPS)
GROUP_FILLED = FIRST.count + (LAYERS - 1) * LAYER.count + HEAD.count
GROUP_MOVED = {e: FIRST.moved[e] + (LAYERS - 1) * LAYER.moved[e] + HEAD.moved[e]
               for e in ("dve", "act")}


def flat(t):
    names = " ".join("abcd"[:len(t.shape) - 1])
    return t.rearrange(f"p {names} -> p ({names})") if len(t.shape) > 2 else t


def across(t, n):
    return t.rearrange("p (a k) -> p a k", a=1).broadcast_to([t.shape[0], n, t.shape[1]])


def along(t, n):
    return t.rearrange("p (k a) -> p k a", a=1).broadcast_to([t.shape[0], t.shape[1], n])


def tower(nc, slots, ident, ident_in, h_dram, x, x_turned, fc0, fc0_t, sw, cwt, cb, fc1_w, fc1_b, fc2_w, fc2_b,
          k_fwd_rows, k_fwd_cols, k_inv_rows, k_inv_cols,
          k_lift_mask):
    with ExitStack() as ctx:
        LB = 128 // (4 * IN_CH)

        def sb(name, shape, dt=F32):
            return ctx.enter_context(nc.sbuf_tensor(name, shape, dt))

        def sem(name):
            return ctx.enter_context(nc.semaphore(name))

        fwd_rows = sb("fwd_rows", [128, PAD_N])
        fwd_cols = sb("fwd_cols", [128, 2, 128])
        inv_rows = sb("inv_rows", [PAD_K, 2, 2, 128], F32R)
        inv_cols = sb("inv_cols", [128, 128])
        lift_w = sb("lift_w", [128, LIFT_E, 4, CH])
        lift_mask = sb("lift_mask", [128, LIFT_E * 4])
        fc0_rows = sb("fc0_rows", [128, CH])
        first_w = sb("first_w", [128, 2, LB, 128], F32R)
        conv_all = sb("conv_all", [128, LAYERS, 128])
        conv_w = sb("conv_w", [128, 2, 128], F32R)
        conv_b_all = sb("conv_b_all", [128, LAYERS])
        conv_b = sb("conv_b", [128, 1])
        w1 = sb("w1", [128, 2, 2, 128], F32R)
        b1 = sb("b1", [128, 1])
        w2 = sb("w2", [128, 32])
        b2 = sb("b2", [128, 1])
        mode_w = sb("mode_w", [128, BLOCKS * MODES, CH])

        act_c = sb("act_c", [128, QUADS, QB, PART])
        big = sb("big", [128, 2, SPATIAL])
        mid = sb("mid", [128, 2, 2, 2, MODES, CH])
        modes = sb("modes", [128, 8, 2 * QUADS, 4 * MODES])
        modes_t = sb("modes_t", [PAD_K, 3, 2, MODES * CH], F32R)
        parts = sb("parts", [128, 2, 2, PART], F32R)

        in_mid = mid[:, 0].rearrange("p r x k c -> p (r x k c)")
        in_mid = in_mid[:, 0:2 * LIFT_T * 32].rearrange("p (r m) -> p r m", r=2)
        xin = mid[:, 0].rearrange("p r x k c -> p (r x k c)")[:, 0:2 * PART].rearrange("p (n m) -> p n m", n=2)
        xin_t = mid[:, 1].rearrange("p r x k c -> p (r x k c)")[:, 0:QUADS * IN_CH * 2 * WW].rearrange(
            "p (q c n) -> p q c n", q=QUADS, c=IN_CH)
        in_modes = mid[:, 1].rearrange("p r x k c -> p (r x k c)")[:, 0:LIFT_T * 32]
        rows = modes[:].rearrange("p m q k -> p (m q k)")[:, 0:2 * SLOT].rearrange("p (b n) -> p b n", b=2)
        fc0_cols = big[:, 0, 0:LB * (128 + 4 * IN_CH)]
        inv_rows_raw = big[0:PAD_K, 1, 256:512].rearrange("p (y n) -> p y n", y=2)
        zeros = big[64:PAD_K, 1, 512:512 + 3 * MODES * CH]
        w1_raw = big[:, 1, 0:256].rearrange("p (j n) -> p j n", j=2)

        filled = sem("filled")
        moved = {"dve": sem("moved_dve"), "act": sem("moved_act")}
        const_in = sem("const_in")
        basis_in = sem("basis_in")
        slots_zeroed = sem("slots_zeroed")
        zeroed = sem("zeroed")
        xin_in = sem("xin_in")
        xin_t_in = sem("xin_t_in")
        first_w_filled = sem("first_w_filled")
        first_w_set = sem("first_w_set")
        mode_w_in = sem("mode_w_in")
        conv_w_set = sem("conv_w_set")
        zeros_set = sem("zeros_set")
        high_turned = sem("high_turned")
        parts_set = sem("parts_set")
        high_set = sem("high_set")
        low_set = sem("low_set")
        turned = sem("turned")
        mix_started = sem("mix_started")
        h_out = [sem(f"h_out{b}") for b in range(2)]

        plain = [(fwd_rows, k_fwd_rows), (fwd_cols, k_fwd_cols), (inv_rows_raw, k_inv_rows),
                 (inv_cols, k_inv_cols), (lift_mask, k_lift_mask)]
        blocks = [(fc0_cols[a * CH:(a + 1) * CH, :].rearrange("p (b m) -> p b m", b=LB)
                   [:, :, a * IN_CH:(a + 1) * IN_CH],
                   fc0_t.rearrange("c (a k) -> c a k", a=1).broadcast_to([CH, LB, IN_CH]))
                  for a in range(4)]
        blocks += [(fc0_rows[:, :], fc0)]
        blocks += [(conv_all[b * CH:(b + 1) * CH, :, b * CH:(b + 1) * CH],
                    cwt.rearrange("l c o -> c l o")) for b in range(QB)]
        blocks += [(w1_raw[b * CH:(b + 1) * CH, b // 2, (b % 2) * HID:(b % 2 + 1) * HID], fc1_w)
                   for b in range(QB)]
        blocks += [(w2[b * HID:(b + 1) * HID, b:b + 1], fc2_w) for b in range(2)]
        columns = [(conv_b_all[b * CH:(b + 1) * CH, :], cb)
                   for b in range(QB)]
        columns += [(b1[b * HID:(b + 1) * HID, :], fc1_b.rearrange("(c a) -> c a", a=1))
                    for b in range(2)]
        columns += [(b2[:, :], fc2_b.rearrange("(a c) -> a c", a=1).broadcast_to([128, 1]))]
        BASES = 16 * len(plain)
        CONSTS = 16 * (len(blocks) + len(columns))

        GROUP_PARTS = 2 + LAYERS * GB
        TURNS = 2 * QUADS * (LAYERS - 1) + 2
        SW_FIRST, SW_SECOND = LAYERS - 2, LAYERS - 1
        block = ctx.enter_context(nc.Block())

        @block.sync
        def _(sp):
            for dst, src in plain:
                sp.dma_start(flat(dst[:] if dst is not inv_rows_raw else dst), src).then_inc(basis_in, 16)
            sp.dma_start(flat(xin_t), x_turned[GROUPS - 1]).then_inc(xin_t_in, 16)
            sp.wait_ge(zeroed, 1)
            for dst, src in blocks + columns:
                sp.dma_start(dst, src).then_inc(const_in, 16)
            sp.dma_start(flat(mode_w[:]), sw[SW_FIRST]).then_inc(mode_w_in, 16)
            with sp.Fori(0, GROUPS) as g:
                sp.wait_ge(filled, g * GROUP_FILLED + EARLY.count)
                sp.dma_start(xin, x[g].rearrange("(n p) m -> p n m", n=2)).then_inc(xin_in, 16)
                sp.wait_ge(filled, g * GROUP_FILLED + EARLY.count + (FIRST.index["mix", 0, BLOCKS - 1] + 1))
                sp.dma_start(flat(mode_w[:]), sw[SW_SECOND]).then_inc(mode_w_in, 16)
                with sp.Fori(0, LAYERS - 1) as l:
                    start = g * GROUP_FILLED + EARLY.count + FIRST.count + l * LAYER.count
                    sp.wait_ge(filled, start + (LAYER.index["mix", 0, BLOCKS - 1] + 1))
                    sp.dma_start(flat(mode_w[:]), sw[l]).then_inc(mode_w_in, 16)
                sp.dma_start(flat(xin_t), x_turned[g]).then_inc(xin_t_in, 16)
                for pair in range(2 * QUADS):
                    _, n = HEAD.moved_at(HEAD.index["fc2", pair, 0])
                    sp.wait_ge(moved["dve"], g * GROUP_MOVED["dve"] + EARLY.moved["dve"] + (
                        FIRST.moved["dve"] + (LAYERS - 1) * LAYER.moved["dve"] + n))
                    for a in range(2):
                        for half in range(2):
                            dst = h_dram.rearrange("(s a r) (g q) m -> g q a s r m", s=2, a=4, g=GROUPS)[
                                g, pair // 2, pair % 2 * 2 + a, half].rearrange("r (b w) -> b r w", b=QB)
                            src = rows[a:128:32, pair % 2, :].rearrange("b (r s w) -> b s r w", r=8, s=2)
                            sp.dma_start(dst, src[:, half]).then_inc(h_out[pair % 2], 16)
            for b in range(2):
                sp.wait_ge(h_out[b], GROUPS * 16 * GB + 1)
            sp.wait_ge(mode_w_in, 16 * (1 + GROUPS * LAYERS))
            sp.wait_ge(xin_in, 16 * GROUPS)
            sp.wait_ge(xin_t_in, 16 * (1 + GROUPS))

        def slot_of(steps, k):
            return slots[:, (steps.first_slot + k) % SLOTS, :]

        def turn_modes(s, q, x, kb):
            return nc.tensor.transpose(s[0:4 * MODES, kb * 128:(kb + 1) * 128],
                                       modes[:, kb, 2 * q + x, :], ident[:, :])

        def layer_pe(s, stage, q, i, first=False):
            if stage == "in_rows":
                for j in range(IN_CH):
                    mm = nc.tensor.matmul(s[:, j * 128:j * 128 + PAD_N], xin_t[:, q, j, :],
                                          fwd_rows[:, :], start=True, stop=True)
            elif stage == "in_cols":
                n = LIFT_T * 32 // 4
                for r in range(2):
                    mm = nc.tensor.matmul(s[:, 0:n], fwd_cols[:, r, :], in_mid[:, r, i * n:(i + 1) * n],
                                          start=(r == 0), stop=(r == 1))
            elif stage == "lift":
                for j in range(2):
                    rhs = in_modes.rearrange("p (t m) -> p t m", m=32)[:, :, 0:4 * BLOCKS]
                    mm = nc.tensor.matmul(s[:, j * 512:j * 512 + LIFT_T * 4 * BLOCKS],
                                          lift_w[:, 2 * i + j].rearrange("p j c -> p (j c)"), rhs,
                                          start=True, stop=True)
            elif stage == "fwd_rows":
                xt = big[:, q % 2, :].rearrange("p (c m) -> p c m", c=CH)
                for j in range(8):
                    mm = nc.tensor.matmul(s[:, j * 128:j * 128 + PAD_N], xt[:, 8 * i + j, :],
                                          fwd_rows[:, :], start=True, stop=True)
            elif stage == "fwd_cols":
                x, first_kh, end_kh = COLS_PARTS[i]
                base, end = first_kh * CH, end_kh * CH
                for lo, hi in ((base, min(end, base + 512)), (base + 512, end)):
                    for r in range(2 if lo < hi else 0):
                        src = mid[:, q % 2, r, x, :, :].rearrange("p k c -> p (k c)")
                        mm = nc.tensor.matmul(s[:, lo - base:hi - base], fwd_cols[:, r, :], src[:, lo:hi],
                                              start=(r == 0), stop=(r == 1))
            elif stage == "mix":
                for kh in range(MODES):
                    for j in range(4):
                        rows_j = slice(j * CH, (j + 1) * CH)
                        mm = nc.tensor.matmul(s[rows_j, kh * 32:(kh + 1) * 32],
                                              mode_w[rows_j, i * MODES + kh, :],
                                              modes[rows_j, i, :, 4 * kh:4 * kh + 4],
                                              start=True, stop=True)
            elif stage == "modes_turn":
                for kb in range(BLOCKS):
                    mm = turn_modes(s, q, i, kb)
            elif stage == "inv_rows":
                half = MODES * CH // 2
                for j in range(2):
                    for n, (u, v) in enumerate(((0, 0), (0, 1), (1, 0))):
                        mm = nc.tensor.matmul(
                            s[:, j * 512:j * 512 + half], inv_rows[:, u, i % 2, :],
                            modes_t[:, (2 * q + i // 2) % 3, v, j * half:(j + 1) * half],
                            start=(n == 0), stop=(n == 2))
            elif stage == "out":
                v = big[:, q % 2, :].rearrange("p (b r m) -> p b r m", b=QB, r=8)
                b = QB * q + i
                for j in range(2):
                    cols = slice(j * 512, (j + 1) * 512)
                    terms = [(first_w[:, u, b % LB, :], parts[:, b // LB, v, cols]) if first else
                             (conv_w[:, u, :], parts[:, b % 2, v, cols]) for u, v in ((0, 0), (0, 1), (1, 0))]
                    for n, (w, src) in enumerate(terms):
                        nc.tensor.matmul(s[:, cols], w, src, start=(n == 0), stop=False,
                                         skip_group_check=True)
                    for h in range(4):
                        r = 4 * j + h
                        mm = nc.tensor.matmul(s[:, r * 128:(r + 1) * 128], v[:, i, r, :], inv_cols[:, :],
                                              start=False, stop=(h == 3), skip_group_check=True)
            return mm

        def head_pe(s, stage, pair, i):
            if stage in ("in_rows", "in_cols"):
                return layer_pe(s, stage, pair, i)
            if stage == "fc1":
                for j in range(2):
                    for n, (u, v) in enumerate(((0, 0), (0, 1), (1, 0))):
                        mm = nc.tensor.matmul(s[:, j * 512:(j + 1) * 512], w1[:, u, pair % 2, :],
                                              parts[:, i % 2, v, j * 512:(j + 1) * 512],
                                              start=(n == 0), stop=(n == 2))
            else:
                for u in range(2):
                    for b in range(QB):
                        at = b * PART + u * 512
                        mm = nc.tensor.matmul(s[32 * b:32 * b + 32, u * 512:(u + 1) * 512], w2[:, :],
                                              big[:, pair % 2, at:at + 512], start=True, stop=True)
            return mm

        FIRST_TURNS = [(0, 0), (0, 1), (1, 0)]

        READS = {"fwd_cols": "fwd_rows"}

        def layer_program(pe, steps, at, first, mode_w_count, conv_w_count, turned_before,
                          parts_before):
            for k, (stage, q, i) in enumerate(steps.steps):
                if k >= SLOTS:
                    e, n = steps.moved_at(k - SLOTS)
                    pe.wait_ge(moved[e], at[e] + n)
                elif not first:
                    pe.wait_ge(moved["act"], at["act"] - (SLOTS - 1 - k))
                if stage == "modes_turn" and (q, i) in FIRST_TURNS:
                    for kb in range(BLOCKS - 1):
                        if (q, i, kb) == (0, 0, 0):
                            for part in range(BLOCKS - 1):
                                e, n = steps.moved_at(steps.index["mix", 0, part])
                                pe.wait_ge(moved[e], at[e] + n)
                        turn_modes(slot_of(steps, k), q, i, kb)
                    if (q, i) != FIRST_TURNS[-1]:
                        continue
                    e, n = steps.moved_at(steps.index["mix", 0, BLOCKS - 1])
                    pe.wait_ge(moved[e], at[e] + n)
                    for early in FIRST_TURNS:
                        s = slot_of(steps, steps.index[("modes_turn",) + early])
                        turn_modes(s, *early, BLOCKS - 1).then_inc(filled, 1)
                    continue
                if stage in READS and i == (2 if (stage, q) == ("fwd_cols", QUADS - 1) else 0):
                    for e, n in steps.outputs_of(READS[stage], q if stage == "fwd_cols" else 0):
                        pe.wait_ge(moved[e], at[e] + n)
                if stage == "fwd_rows" and i == 0:
                    pe.wait_ge(turned, turned_before + (2 * q + 2))
                if stage == "inv_rows":
                    e, n = steps.moved_at(steps.index["modes_turn", q, i // 2])
                    pe.wait_ge(moved[e], at[e] + n)
                if stage == "out":
                    e, n = steps.moved_at(steps.index["inv_rows", q, i])
                    pe.wait_ge(moved[e], at[e] + n)
                if stage == "mix" and i == 0:
                    for e, n in (steps.outputs_of("lift", 0) if first
                                 else steps.outputs_of("fwd_cols", QUADS - 1)):
                        pe.wait_ge(moved[e], at[e] + n)
                    pe.wait_ge(mode_w_in, mode_w_count)
                if (stage, q, i) == ("out", 0, 0) and not first:
                    pe.wait_ge(conv_w_set, conv_w_count)
                if stage == "mix":
                    pe.sem_inc(mix_started, 1)
                if stage == "out":
                    n = (QB * q + i) // LB + 1 if first else QB * q + i + 1
                    pe.wait_ge(high_set, parts_before + n)
                    pe.wait_ge(low_set, parts_before + n)
                layer_pe(slot_of(steps, k), stage, q, i, first).then_inc(filled, 1)

        @block.tensor
        def _(pe):
            pe.wait_ge(basis_in, BASES)
            pe.wait_ge(slots_zeroed, 1)
            pe.wait_ge(xin_t_in, 16)
            for k, (stage, q, i) in enumerate(EARLY.steps):
                if (stage, i) == ("in_cols", 0):
                    for quad in (QUADS - 2, QUADS - 1):
                        e, n = EARLY.moved_at(EARLY.index["in_rows", quad, 0])
                        pe.wait_ge(moved[e], n)
                layer_pe(slot_of(EARLY, k), stage, q, i).then_inc(filled, 1)
            for e in moved:
                pe.wait_ge(moved[e], EARLY.moved[e])
            pe.wait_ge(const_in, CONSTS)
            pe.wait_ge(ident_in, 16)
            for b in range(LB):
                mm = nc.tensor.matmul(slots[:, 0, :][:, b * 128:(b + 1) * 128],
                                      fc0_cols[:, b * 128:(b + 1) * 128], conv_all[:, LAYERS - 1, :],
                                      start=True, stop=True)
            mm.then_inc(first_w_filled, 1)
            pe.wait_ge(first_w_set, 3)
            pe.wait_ge(parts_set, 4)
            with pe.Fori(0, GROUPS) as g:
                at = {e: g * GROUP_MOVED[e] + EARLY.moved[e] for e in moved}
                layer_program(pe, FIRST, at, True, g * (16 * LAYERS) + 16, None, None, g * GROUP_PARTS)
                with pe.Fori(0, LAYERS - 1) as l:
                    at = {e: g * GROUP_MOVED[e] + l * LAYER.moved[e] + (EARLY.moved[e] + FIRST.moved[e])
                          for e in moved}
                    layer_program(pe, LAYER, at, False, g * (16 * LAYERS) + l * 16 + 32,
                                  g * (3 * LAYERS - 2) + l * 3 + 4, g * TURNS + l * (2 * QUADS),
                                  g * GROUP_PARTS + l * GB + 2)
                base = {e: FIRST.moved[e] + (LAYERS - 1) * LAYER.moved[e] for e in moved}
                at = {e: g * GROUP_MOVED[e] + EARLY.moved[e] for e in moved}
                for k, (stage, pair, i) in enumerate(HEAD.steps):
                    if k >= SLOTS:
                        e, n = HEAD.moved_at(k - SLOTS)
                        pe.wait_ge(moved[e], at[e] + (base[e] + n))
                    else:
                        pe.wait_ge(moved["act"], at["act"] + (base["act"] - (SLOTS - 1 - k)))
                    if stage == "fc1" and pair % 2 == 0:
                        n = 2 + (LAYERS - 1) * GB + QB * (pair // 2) + i + 1
                        pe.wait_ge(high_set, g * GROUP_PARTS + n)
                        pe.wait_ge(low_set, g * GROUP_PARTS + n)
                    if stage == "fc2":
                        for e, n in HEAD.outputs_of("fc1", pair):
                            pe.wait_ge(moved[e], at[e] + (base[e] + n))
                    if (stage, i) == ("in_cols", 0):
                        for quad in (QUADS - 2, QUADS - 1):
                            e, n = HEAD.moved_at(HEAD.index["in_rows", quad, 0])
                            pe.wait_ge(moved[e], at[e] + (base[e] + n))
                    if (stage, pair) == ("in_rows", 0):
                        pe.wait_ge(xin_t_in, g * 16 + 32)
                    head_pe(slot_of(HEAD, k), stage, pair, i).then_inc(filled, 1)
                for e in moved:
                    pe.wait_ge(moved[e], at[e] + (base[e] + HEAD.moved[e]))

        def plain_move(engine, dst, src):
            if engine == "dve":
                return nc.vector.tensor_copy(dst, src)
            return nc.scalar.copy(dst, src)

        def move(engine, s, stage, q, i):
            if stage == "in_rows":
                src = s[:, 0:512].rearrange("p (c n) -> p c n", c=IN_CH)[:, :, 0:4 * MODES]
                dst = in_mid.rearrange("p r (q k c) -> p q c k r", q=QUADS, c=IN_CH)[:, q]
                return plain_move(engine, dst, src.rearrange("p c (k r) -> p c k r", r=2))
            if stage == "in_cols":
                n = LIFT_T * 32 // 4
                return nc.vector.transpose(in_modes[:, i * n:(i + 1) * n], s[:, 0:n])
            if stage == "lift":
                to = modes[:, 0:BLOCKS].rearrange("p m q k -> p m (q k)").rearrange(
                    "p m (t e b) -> p e t m b", e=LIFT_E, b=4)
                for j in range(2):
                    src = s[:, j * 512:j * 512 + LIFT_T * 4 * BLOCKS].rearrange(
                        "p (t m b) -> p t m b", m=BLOCKS, b=4)
                    last = plain_move(engine, to[:, 2 * i + j], src)
                return last
            if stage == "fwd_rows":
                dst = mid[:, q % 2, :, :, :, 8 * i:8 * i + 8].rearrange("p r x k c -> p c (x k) r")
                src = s.rearrange("p (c n) -> p c n", c=8)[:, :, 0:4 * MODES]
                return plain_move(engine, dst, src.rearrange("p c (k r) -> p c k r", r=2))
            if stage == "fwd_cols":
                x, lo, hi = COLS_PARTS[i]
                dst = modes[:, :, 2 * q + x, :].rearrange("p m (k b) -> p k m b", b=4)
                return nc.vector.transpose(dst[:, lo:hi], s[:, 0:(hi - lo) * CH])
            if stage == "mix":
                dst = modes[:, i, :, :].rearrange("p q (k b) -> p k q b", b=4)
                return plain_move(engine, dst, s[:, 0:MODES * 32].rearrange(
                    "p (k q b) -> p k q b", k=MODES, b=4))
            if stage == "modes_turn":
                high, low = (modes_t[0:4 * MODES, (2 * q + i) % 3, n, :] for n in range(2))
                src = s[0:4 * MODES, 0:MODES * CH]
                if engine == "act":
                    return nc.scalar.copy(high, src)
                return nc.vector.tensor_tensor(low, src, high.bitcast(F32), ALU.subtract)
            if stage == "inv_rows":
                dst = big[:, q % 2, i * PART:(i + 1) * PART].rearrange("p (r a o) -> p o a r", r=8, a=4)
                return nc.vector.transpose(dst, s.rearrange("p (k o) -> p o k", o=CH))
            if stage == "out":
                return nc.scalar.activation(act_c[:, q, i, :], s, ACT.Gelu,
                                            bias=conv_b[:, 0:1])
            if stage == "fc1":
                return nc.scalar.activation(big[:, q % 2, i * SLOT:(i + 1) * SLOT], s, ACT.Gelu,
                                            bias=b1[:, 0:1])
            if stage == "fc2":
                return nc.vector.tensor_scalar(rows[:, q % 2, :], s, b2[:, 0:1], None, ALU.add)

        def turn(q, y):
            src = act_c[:, q, y:QB:2, :].rearrange("p x (m w) -> p w x m", w=WW)
            dst = big[:, q % 2, :].rearrange("p (c y w) -> p y w c", c=CH, y=2)[:, y]
            return nc.vector.transpose(dst, src)

        def split(engine, eng, n, parts_before, first=False):
            src = xin[:, n, :] if first else act_c[:, n // QB, n % QB, :]
            high, low = parts[:, n % 2, 0, :], parts[:, n % 2, 1, :]
            if engine == "act":
                nc.scalar.copy(high, src).then_inc(high_set, 1)
            elif engine == "both":
                nc.vector.tensor_copy(high, src).then_inc(high_set, 1)
            if engine != "act":
                eng.wait_ge(high_set, parts_before + (n + 1))
                nc.vector.tensor_tensor(low, src, high.bitcast(F32), ALU.subtract).then_inc(low_set, 1)

        def move_layer(engine, eng, steps, at, start, conv_w_count, parts_before, turned_before,
                       first=False, rows_before=None, xin_count=None):
            turns = 0
            for k, (stage, q, i) in enumerate(steps.steps):
                if engine == "dve" and stage == "fwd_rows" and q < QUADS - 2 and i == 3:
                    eng.wait_ge(filled, start + (k + 1))
                    for y in range(2):
                        turn(q + 2, y).then_inc(turned, 1)
                if engine == "dve" and stage == "out" and q == QUADS - 1 and i < 2:
                    _, n = steps.moved_at(steps.index["out", 0, QB - 1])
                    eng.wait_ge(moved["act"], at["act"] + n)
                    eng.wait_ge(filled, start + (steps.index["out", 2, QB - 1] + 1))
                    turn(0, i).then_inc(turned, 1)
                if stage == "lift" and i < 2:
                    for b in range(2):
                        eng.wait_ge(h_out[b], rows_before + 1)
                if stage == "modes_turn" and engine == "act":
                    eng.wait_ge(filled, start + (k + 1))
                    move(engine, slot_of(steps, k), stage, q, i).then_inc(high_turned, 1)
                elif stage == "modes_turn":
                    turns += 1
                    eng.wait_ge(high_turned, turned_before + turns)
                if steps.by[k] == engine:
                    if (stage, q, i) == ("out", 0, 0):
                        eng.wait_ge(conv_w_set, conv_w_count)
                    eng.wait_ge(filled, start + (k + 1))
                    move(engine, slot_of(steps, k), stage, q, i).then_inc(moved[engine], 1)
                if (stage, i) == ("mix", 3 if engine == "act" else 4):
                    if first:
                        eng.wait_ge(xin_in, xin_count)
                    for n in range(2):
                        split(engine, eng, n, parts_before, first)
                if first:
                    continue
                n = QB * q + i + 2 - (QB if stage == "inv_rows" else 0)
                if n < GB and ((stage == "out" and (engine == "act" or q == QUADS - 1))
                               or (engine == "dve" and stage == "inv_rows" and q > 0)):
                    split(engine, eng, n, parts_before)

        def early_moves(engine, eng):
            for k, (stage, q, i) in enumerate(EARLY.steps):
                if EARLY.by[k] == engine:
                    eng.wait_ge(filled, k + 1)
                    move(engine, slot_of(EARLY, k), stage, q, i).then_inc(moved[engine], 1)

        def mover_program(engine, eng):
            with eng.Fori(0, GROUPS) as g:
                if engine == "dve":
                    nc.vector.tensor_copy(conv_b[:, :],
                                          conv_b_all[:, LAYERS - 1:LAYERS]).then_inc(conv_w_set, 1)
                move_layer(engine, eng, FIRST, {e: g * GROUP_MOVED[e] + EARLY.moved[e] for e in moved},
                           g * GROUP_FILLED + EARLY.count, g * (3 * LAYERS - 2) + 1, g * GROUP_PARTS,
                           g * (LAYERS * 2 * QUADS), True, g * (16 * GB), g * 16 + 16)
                with eng.Fori(0, LAYERS - 1) as l:
                    start = g * GROUP_FILLED + EARLY.count + l * LAYER.count + FIRST.count
                    at = {e: g * GROUP_MOVED[e] + l * LAYER.moved[e] + (EARLY.moved[e] + FIRST.moved[e])
                          for e in moved}
                    if engine == "dve":
                        eng.wait_ge(moved["act"], at["act"])
                        for y in range(2):
                            turn(1, y).then_inc(turned, 1)
                        nc.vector.tensor_copy(conv_b[:, :],
                                              conv_b_all[:, bass.ds(l, 1)]).then_inc(conv_w_set, 1)
                        layer_w = conv_all[:, bass.ds(l, 1), :].rearrange("p a n -> p (a n)")
                        nc.vector.tensor_copy(conv_w[:, 0, :], layer_w).then_inc(conv_w_set, 1)
                        eng.wait_ge(conv_w_set, g * (3 * LAYERS - 2) + l * 3 + 3)
                        nc.vector.tensor_tensor(conv_w[:, 1, :], layer_w, conv_w[:, 0, :].bitcast(F32),
                                                ALU.subtract).then_inc(conv_w_set, 1)
                    move_layer(engine, eng, LAYER, at, start, g * (3 * LAYERS - 2) + l * 3 + 4,
                               g * GROUP_PARTS + l * GB + 2,
                               g * (LAYERS * 2 * QUADS) + l * (2 * QUADS) + 2 * QUADS)
                start = FIRST.count + (LAYERS - 1) * LAYER.count
                parts_before = g * GROUP_PARTS + (2 + (LAYERS - 1) * GB)
                if engine == "dve":
                    for n in range(2):
                        eng.wait_ge(filled, g * GROUP_FILLED + EARLY.count + (start - 1 + n))
                        split("both", eng, n, parts_before)
                    eng.wait_ge(moved["act"], g * GROUP_MOVED["act"] + EARLY.moved["act"] + (
                        FIRST.moved["act"] + (LAYERS - 1) * LAYER.moved["act"]))
                for k, (stage, q, i) in enumerate(HEAD.steps):
                    n = QB * (q // 2) + i + 2
                    if engine == "dve" and stage == "fc1" and q % 2 and n < GB:
                        eng.wait_ge(filled, g * GROUP_FILLED + EARLY.count + (start + k + 1))
                        split("both", eng, n, parts_before)
                    if HEAD.by[k] == engine:
                        if stage == "fc2" and q >= 2:
                            eng.wait_ge(h_out[q % 2], g * (16 * GB) + (64 * (q // 2) + 1))
                        if (stage, q, i) == ("fc1", 0, 0):
                            eng.wait_ge(turned, g * TURNS + TURNS)
                        last = k
                        if stage == "fc1" and q >= 2:
                            last = max(k, HEAD.index["fc2", q - 2, 0])
                        eng.wait_ge(filled, g * GROUP_FILLED + EARLY.count + (start + last + 1))
                        move(engine, slot_of(HEAD, k), stage, q, i).then_inc(moved[engine], 1)

        @block.vector
        def _(dve):
            nc.vector.memset(fc0_cols, 0.0)
            nc.vector.memset(conv_all[:], 0.0)
            nc.vector.memset(w1_raw, 0.0)
            nc.vector.memset(w2[:], 0.0)
            dve.drain().then_inc(zeroed, 1)
            nc.vector.memset(slots[:, :, :], 0.0).then_inc(slots_zeroed, 1)
            nc.vector.memset(zeros, 0.0).then_inc(zeros_set, 1)
            dve.wait_ge(zeros_set, 1)
            for n in range(2):
                nc.vector.tensor_copy(modes_t[64:PAD_K, :, n, :],
                                      zeros.rearrange("p (b n) -> p b n", b=3)).then_inc(zeros_set, 1)
            for b in range(2):
                dve.sem_inc(h_out[b], 1)
            early_moves("dve", dve)
            dve.wait_ge(basis_in, BASES)
            dve.wait_ge(const_in, CONSTS)
            nc.vector.tensor_tensor(
                lift_w[:].rearrange("p e j c -> p (e j) c"), across(fc0_rows[:, :], 4 * LIFT_E),
                along(lift_mask[:, :], CH), ALU.mult).then_inc(first_w_set, 1)
            nc.vector.tensor_copy(inv_rows[:, 0], inv_rows_raw).then_inc(parts_set, 1)
            nc.vector.tensor_copy(w1[:, 0], w1_raw).then_inc(parts_set, 1)
            dve.wait_ge(parts_set, 2)
            nc.vector.tensor_tensor(inv_rows[:, 1], inv_rows_raw, inv_rows[:, 0].bitcast(F32),
                                    ALU.subtract).then_inc(parts_set, 1)
            nc.vector.tensor_tensor(w1[:, 1], w1_raw, w1[:, 0].bitcast(F32),
                                    ALU.subtract).then_inc(parts_set, 1)
            dve.wait_ge(first_w_filled, 1)
            nc.vector.tensor_copy(flat(first_w[:, 0]), slots[:, 0, :]).then_inc(first_w_set, 1)
            dve.wait_ge(first_w_set, 2)
            nc.vector.tensor_tensor(flat(first_w[:, 1]), slots[:, 0, :], flat(first_w[:, 0]).bitcast(F32),
                                    ALU.subtract).then_inc(first_w_set, 1)
            mover_program("dve", dve)

        @block.scalar
        def _(act):
            early_moves("act", act)
            act.wait_ge(const_in, CONSTS)
            mover_program("act", act)


def centre(nc, link, src, centred, squares, stats):
    link(nc.vector.tensor_reduce(stats[:, 0, :], src, AX_X, ALU.add))
    link(nc.vector.tensor_scalar(stats[:, 1, :], stats[:, 0, :], -1.0 / D, None, ALU.mult))
    link(nc.vector.tensor_tensor(centred, src, along(stats[:, 1, :], D), ALU.add))
    link(nc.vector.tensor_tensor(squares, centred, centred, ALU.mult))
    link(nc.vector.tensor_reduce(stats[:, 0, :], squares, AX_X, ALU.add))
    return nc.vector.tensor_scalar(stats[:, 1, :], stats[:, 0, :], 1.0 / D, EPS, ALU.mult, ALU.add)


def root(nc, stats):
    return nc.scalar.activation(stats[:, 2, :], stats[:, 1, :], ACT.Sqrt)


def invert_root(nc, link, stats):
    link(nc.vector.reciprocal(stats[:, 0, :], stats[:, 2, :]))
    link(nc.vector.tensor_tensor(stats[:, 0, :], stats[:, 0, :], stats[:, 1, :], ALU.mult))
    link(nc.vector.tensor_tensor(stats[:, 0, :], stats[:, 0, :], stats[:, 2, :], ALU.add))
    link(nc.vector.tensor_scalar(stats[:, 1, :], stats[:, 0, :], 0.5, None, ALU.mult))
    link(nc.vector.reciprocal(stats[:, 2, :], stats[:, 1, :]))


ATTENTION = Steps([("x_turn", 0, c) for c in range(4)] + [("qkv", 0, c) for c in range(8)]
                  + [("qk_turn", k, c) for c in range(4) for k in range(2)]
                  + [("scores", 0, c) for c in range(4)] + [("attend", 0, c) for c in range(2)])
ROUTING = Steps([("y_turn", 0, c) for c in range(4)] + [("gate", 0, c) for c in range(4)]
                + [("s_turn", 0, c) for c in range(4)])


PARTS = [slice(0, TILES // 2), slice(TILES // 2, TILES)]


def attention(nc, slots, ident, h2, h_dram, wqkv, k_rope, k_decay):
    with ExitStack() as ctx:
        def sb(name, shape, dt=F32):
            return ctx.enter_context(nc.sbuf_tensor(name, shape, dt))

        def sem(name):
            return ctx.enter_context(nc.semaphore(name))

        h = sb("at_h", [128, TILES, D])
        centred = sb("at_centred", [128, TILES, D])
        squares = sb("at_squares", [128, TILES, D])
        normed = sb("at_normed", [128, TILES, D])
        stats = sb("at_stats", [128, 3, TILES])
        w = sb("at_w", [D, 3 * D])
        rope = sb("at_rope", [128, 4, D])
        decay = sb("at_decay", [128, 128])
        normed_t = sb("at_normed_t", [D, TOKENS])
        qkv = sb("at_qkv", [128, TILES, 3 * D])
        turned = sb("at_turned", [128, 2, TILES, D])
        qk_t = sb("at_qk_t", [D, 2, TOKENS])
        ret_t = sb("at_ret_t", [128, TILES, 128])

        h_in = [sem(f"at_h_in{n}") for n in range(2)]
        weights_in = sem("at_weights_in")
        chain = sem("at_chain")
        norm_done = sem("at_norm_done")
        variance_done = sem("at_variance_done")
        root_done = sem("at_root_done")
        rope_done = sem("at_rope_done")
        filled = sem("at_filled")
        moved = {"dve": sem("at_moved_dve"), "act": sem("at_moved_act")}
        block = ctx.enter_context(nc.Block())

        @block.sync
        def _(sp):
            src = h_dram.rearrange("h q (y x w) -> x h (q y) w", y=2, x=2)
            for n, tiles in enumerate(PARTS):
                for x in range(2):
                    sp.dma_start(h[x * HH:(x + 1) * HH, tiles], src[x][:, tiles]).then_inc(h_in[n], 16)
            sp.dma_start(w[:], wqkv).then_inc(weights_in, 16)
            sp.dma_start(flat(rope[:]), k_rope).then_inc(weights_in, 16)
            sp.dma_start(decay[:], k_decay).then_inc(weights_in, 16)

        @block.tensor
        def _(pe):
            pe.wait_ge(weights_in, 48)
            for k, (stage, q, i) in enumerate(ATTENTION.steps):
                s = slots[:, k % SLOTS, :]
                if k >= SLOTS:
                    e, n = ATTENTION.moved_at(k - SLOTS)
                    pe.wait_ge(moved[e], n)
                if stage == "x_turn" and i % 2 == 0:
                    pe.wait_ge(norm_done, i // 2 + 1)
                if (stage, i) == ("qkv", 0):
                    for e, n in ATTENTION.outputs_of("x_turn", 0):
                        pe.wait_ge(moved[e], n)
                if (stage, i) == ("qk_turn", 0):
                    pe.wait_ge(rope_done, q + 1)
                if (stage, i) == ("scores", 0):
                    for part in range(2):
                        for e, n in ATTENTION.outputs_of("qk_turn", part):
                            pe.wait_ge(moved[e], n)
                if (stage, i) == ("attend", 0):
                    for e, n in ATTENTION.outputs_of("scores", 0):
                        pe.wait_ge(moved[e], n)
                if stage == "x_turn":
                    for j in range(8):
                        mm = nc.tensor.transpose(s[0:D, j * 128:(j + 1) * 128],
                                                 normed[:, 8 * i + j, :], ident[:, :])
                elif stage == "qkv":
                    for j in range(4):
                        at = (4 * i + j) * 128
                        mm = nc.tensor.matmul(s[:, j * 256:j * 256 + 3 * D], normed_t[:, at:at + 128],
                                              w[:, :], start=True, stop=True)
                elif stage == "qk_turn":
                    for j in range(8):
                        mm = nc.tensor.transpose(s[0:D, j * 128:(j + 1) * 128],
                                                 turned[:, q, 8 * i + j, :], ident[:, :])
                elif stage == "scores":
                    for j in range(8):
                        at = (8 * i + j) * 128
                        mm = nc.tensor.matmul(s[:, j * 128:(j + 1) * 128], qk_t[:, 1, at:at + 128],
                                              qk_t[:, 0, at:at + 128], start=True, stop=True)
                else:
                    for j in range(16):
                        t = 16 * i + j
                        mm = nc.tensor.matmul(s[:, j * D:(j + 1) * D], ret_t[:, t, :],
                                              qkv[:, t, 2 * D:3 * D], start=True, stop=True)
                mm.then_inc(filled, 1)

        def mover_program(engine, eng):
            for k, (stage, q, i) in enumerate(ATTENTION.steps):
                if ATTENTION.by[k] != engine:
                    continue
                s = slots[:, k % SLOTS, :]
                if engine == "dve" and (stage, q, i) == ("qk_turn", 0, 0):
                    rotate(eng)
                eng.wait_ge(filled, k + 1)
                if stage == "x_turn":
                    dst, src = normed_t[:, i * SLOT:(i + 1) * SLOT], s[0:D, :]
                elif stage == "qkv":
                    dst = qkv[:, 4 * i:4 * i + 4, :]
                    src = s.rearrange("p (t n) -> p t n", t=4)[:, :, 0:3 * D]
                elif stage == "qk_turn":
                    dst, src = qk_t[:, q, i * SLOT:(i + 1) * SLOT], s[0:D, :]
                if stage == "scores":
                    ins = nc.vector.tensor_tensor(ret_t[:, 8 * i:8 * i + 8, :],
                                                  s.rearrange("p (t n) -> p t n", t=8),
                                                  across(decay[:, :], 8), ALU.mult)
                elif stage == "attend":
                    ins = nc.vector.tensor_tensor(h2[:, 16 * i:16 * i + 16, :],
                                                  s.rearrange("p (t n) -> p t n", n=D),
                                                  h[:, 16 * i:16 * i + 16, :], ALU.add)
                elif engine == "dve":
                    ins = nc.vector.tensor_copy(dst, src)
                else:
                    ins = nc.scalar.copy(dst, src)
                ins.then_inc(moved[engine], 1)

        steps = [0]

        def rotate(dve):
            for e, n in ATTENTION.outputs_of("qkv", 0):
                dve.wait_ge(moved[e], n)
            for k in range(2):
                src = qkv[:, :, k * D:(k + 1) * D]
                cos, sin = rope[:, 2 * k, :], rope[:, 2 * k + 1, :]
                nc.vector.tensor_tensor(centred[:], src, across(cos, TILES), ALU.mult)
                swapped = squares[:].rearrange("p t (i r) -> p t i r", r=2)
                pairs = src.rearrange("p t (i r) -> p t i r", r=2)
                for r in range(2):
                    table = sin.rearrange("p (i r) -> p i r", r=2)[:, :, r]
                    steps[0] += 1
                    nc.vector.tensor_tensor(swapped[:, :, :, r], pairs[:, :, :, 1 - r],
                                            across(table, TILES), ALU.mult).then_inc(chain, 1)
                dve.wait_ge(chain, steps[0])
                nc.vector.tensor_tensor(turned[:, k, :, :], centred[:], squares[:],
                                        ALU.add).then_inc(rope_done, 1)
                dve.wait_ge(rope_done, k + 1)

        @block.vector
        def _(dve):
            def link(ins):
                steps[0] += 1
                ins.then_inc(chain, 1)
                dve.wait_ge(chain, steps[0])

            for n, tiles in enumerate(PARTS):
                dve.wait_ge(h_in[n], 32)
                centre(nc, link, h[:, tiles], centred[:, tiles], squares[:, tiles],
                       stats[:, :, tiles]).then_inc(variance_done, 1)
            for n, tiles in enumerate(PARTS):
                dve.wait_ge(root_done, n + 1)
                invert_root(nc, link, stats[:, :, tiles])
                nc.vector.tensor_tensor(normed[:, tiles], centred[:, tiles],
                                        along(stats[:, 2, tiles], D), ALU.mult).then_inc(norm_done, 1)
            dve.wait_ge(norm_done, 2)
            dve.wait_ge(weights_in, 48)
            mover_program("dve", dve)

        @block.scalar
        def _(act):
            for n, tiles in enumerate(PARTS):
                act.wait_ge(variance_done, n + 1)
                root(nc, stats[:, :, tiles]).then_inc(root_done, 1)
            mover_program("act", act)


GUARD = 3.0e38


def experts(nc, slots, ident, h2, gate_t, lattice, out_wt, out_b, ln_g, ln_b, k_select, out):
    with ExitStack() as ctx:
        def sb(name, shape, dt=F32):
            return ctx.enter_context(nc.sbuf_tensor(name, shape, dt))

        def sem(name):
            return ctx.enter_context(nc.semaphore(name))

        EB = EXPERTS // 2
        PB = 3
        y2 = sb("ex_y2", [128, TILES, 2, D])
        centred = sb("ex_centred", [128, TILES, D])
        squares = sb("ex_squares", [128, TILES, D])
        stats = sb("ex_stats", [128, 3, TILES])
        gate_w = sb("ex_gate_w", [128, PAD_N])
        lattice_w = sb("ex_lattice_w", [128, EB, D])
        out_w = sb("ex_out_w", [128, D])
        vectors = sb("ex_vectors", [128, 3, D])
        y_t = sb("ex_y_t", [128, TOKENS])
        logits = sb("ex_logits", [128, TILES, EXPERTS + 2])
        top = sb("ex_top", [128, TILES, 8])
        level = sb("ex_level", [128, TILES, EXPERTS])
        taken = sb("ex_taken", [128, TILES, EXPERTS + 2])
        halves = sb("ex_halves", [128, TILES, 2, EXPERTS])
        halves_t = sb("ex_halves_t", [128, TOKENS], F32R)
        select = sb("ex_select", [128, EB * 128], F32R)
        select_raw = sb("ex_select_raw", [128, EB * 128])
        weighted = sb("ex_weighted", [128, PB, SLOT])
        mixed = sb("ex_mixed", [128, 4, 512])

        weights_in = sem("ex_weights_in")
        zeroed = sem("ex_zeroed")
        select_in = sem("ex_select_in")
        select_set = sem("ex_select_set")
        lattice_in = sem("ex_lattice_in")
        chain = sem("ex_chain")
        norm_done = sem("ex_norm_done")
        variance_done = sem("ex_variance_done")
        root_done = sem("ex_root_done")
        copied = sem("ex_copied")
        shifted = sem("ex_shifted")
        exp_done = sem("ex_exp_done")
        halves_done = sem("ex_halves_done")
        filled = sem("ex_filled")
        moved = {"dve": sem("ex_moved_dve"), "act": sem("ex_moved_act")}
        spread = sem("ex_spread")
        weigh = sem("ex_weigh")
        summed = sem("ex_summed")
        mixed_out = sem("ex_mixed_out")
        projected = sem("ex_projected")
        result = sem("ex_result")
        stored = sem("ex_stored")
        block = ctx.enter_context(nc.Block())

        @block.sync
        def _(sp):
            for half in range(2):
                sp.dma_start(out_w[half * D:(half + 1) * D, :], out_wt).then_inc(weights_in, 16)
            for n, v in enumerate((out_b, ln_g, ln_b)):
                sp.dma_start(vectors[:, n, :], v.rearrange("(a d) -> a d", a=1).broadcast_to(
                    [128, D])).then_inc(weights_in, 16)
            sp.wait_ge(zeroed, 1)
            sp.dma_start(gate_w[0:D, 0:EXPERTS], gate_t).then_inc(weights_in, 16)
            sp.dma_start(select_raw[:], k_select).then_inc(select_in, 16)
            sp.dma_start(flat(lattice_w[:]), lattice).then_inc(lattice_in, 16)
            for n, tiles in enumerate(PARTS):
                sp.wait_ge(result, n + 1)
                sp.dma_start(out.rearrange("(t b) h w -> (b h) t w", b=2)[:, tiles],
                             squares[:, tiles]).then_inc(stored, 16)
            sp.wait_ge(stored, 32)

        @block.tensor
        def _(pe):
            pe.wait_ge(weights_in, 96)
            for k, (stage, q, i) in enumerate(ROUTING.steps):
                s = slots[:, k % SLOTS, :]
                if k >= SLOTS:
                    e, n = ROUTING.moved_at(k - SLOTS)
                    pe.wait_ge(moved[e], n)
                if stage == "y_turn" and i % 2 == 0:
                    pe.wait_ge(norm_done, i // 2 + 1)
                    pe.wait_ge(copied, i // 2 + 1)
                if (stage, i) == ("gate", 0):
                    for e, n in ROUTING.outputs_of("y_turn", 0):
                        pe.wait_ge(moved[e], n)
                if (stage, i) == ("s_turn", 0):
                    pe.wait_ge(halves_done, 1)
                for j in range(8):
                    t = 8 * i + j
                    if stage == "gate":
                        mm = nc.tensor.matmul(s[:, j * 128:j * 128 + PAD_N], y_t[:, t * 128:(t + 1) * 128],
                                              gate_w[:, :], start=True, stop=True)
                    else:
                        src = y2 if stage == "y_turn" else halves
                        mm = nc.tensor.transpose(s[:, j * 128:(j + 1) * 128], flat(src[:, t, :, :]),
                                                 ident[:, :])
                mm.then_inc(filled, 1)
            for e in moved:
                pe.wait_ge(moved[e], ROUTING.moved[e])
            pe.wait_ge(select_set, 1)
            pe.wait_ge(lattice_in, 16)
            with pe.Fori(0, 4) as g:
                def spread_block(n):
                    if n >= PB:
                        pe.wait_ge(weigh, g * EB + (n - PB + 1))
                    for j in range(2):
                        mm = nc.tensor.matmul(slots[:, n % PB, j * 512:(j + 1) * 512],
                                              select[:, n * 128:(n + 1) * 128],
                                              halves_t[:, bass.ds(g * SLOT + j * 512, 512)],
                                              start=True, stop=True)
                    mm.then_inc(spread, 1)

                for n in range(PB - 1):
                    spread_block(n)
                for n in range(EB):
                    if n + PB - 1 < EB:
                        spread_block(n + PB - 1)
                    pe.wait_ge(weigh, g * EB + (n + 1))
                    if n == 0:
                        pe.wait_ge(mixed_out, g + 1)
                    for j in range(2):
                        mm = nc.tensor.matmul(slots[j * D:(j + 1) * D, SLOTS - 1, 0:512],
                                              lattice_w[:, n, :], weighted[:, n % PB, j * 512:(j + 1) * 512],
                                              start=(n == 0), stop=(n == EB - 1))
                mm.then_inc(summed, 1)
            pe.wait_ge(mixed_out, 5)
            for i in range(2):
                for j in range(16):
                    t = 16 * i + j
                    half = t % 8 // 4
                    rows = slice(half * D, half * D + D)
                    at = t % 4 * 128
                    to = half * 512 + (j // 8 * 4 + t % 4) * D
                    mm = nc.tensor.matmul(slots[:, i, to:to + D], mixed[rows, t // 8, at:at + 128],
                                          out_w[rows, :], start=True, stop=True)
                mm.then_inc(projected, 1)

        def mover_program(engine, eng):
            for k, (stage, q, i) in enumerate(ROUTING.steps):
                if engine == "dve" and (stage, i) == ("s_turn", 0):
                    route(eng)
                if engine == "act" and (stage, i) == ("gate", 0):
                    eng.wait_ge(select_in, 16)
                    nc.scalar.copy(select[:], select_raw[:]).then_inc(select_set, 1)
                if engine == "act" and (stage, i) == ("s_turn", 0):
                    for n in range(4):
                        eng.wait_ge(shifted, n + 1)
                        part = level[:, 8 * n:8 * n + 8]
                        nc.scalar.activation(part, part, ACT.Exp).then_inc(exp_done, 1)
                if ROUTING.by[k] != engine:
                    continue
                s = slots[:, k % SLOTS, :]
                eng.wait_ge(filled, k + 1)
                if stage == "gate":
                    dst = logits[:, 8 * i:8 * i + 8, 0:EXPERTS]
                    src = s.rearrange("p (t n) -> p t n", t=8)[:, :, 0:EXPERTS]
                else:
                    dst = (y_t if stage == "y_turn" else halves_t)[:, i * SLOT:(i + 1) * SLOT]
                    src = s
                if engine == "dve":
                    nc.vector.tensor_copy(dst, src).then_inc(moved[engine], 1)
                else:
                    nc.scalar.copy(dst, src).then_inc(moved[engine], 1)

        steps = [0]

        def linked(dve):
            def link(ins):
                steps[0] += 1
                ins.then_inc(chain, 1)
                dve.wait_ge(chain, steps[0])
            return link

        def route(dve):
            link = linked(dve)
            for i in range(4):
                tiles = slice(8 * i, 8 * i + 8)
                e, n = ROUTING.moved_at(ROUTING.index["gate", 0, i])
                dve.wait_ge(moved[e], n)
                for t in range(8 * i, 8 * i + 8):
                    last = nc.vector.max(top[:, t, :], logits[:, t, 0:EXPERTS])
                link(last)
                nc.vector.tensor_tensor(level[:, tiles], logits[:, tiles, 0:EXPERTS],
                                        along(top[:, tiles, 0], EXPERTS),
                                        ALU.subtract).then_inc(shifted, 1)
                link(nc.vector.memset(top[:, tiles, TOP_K:8], GUARD))
                for t in range(8 * i, 8 * i + 8):
                    last = nc.vector.match_replace(taken[:, t, :], top[:, t, :], logits[:, t, :], -GUARD)
            link(last)
            dve.wait_ge(exp_done, 4)
            link(nc.vector.scalar_tensor_tensor(squares[:], taken[:, :, 0:EXPERTS], -GUARD, level[:],
                                                ALU.is_equal, ALU.mult))
            link(nc.vector.tensor_reduce(stats[:, 0, :], squares[:], AX_X, ALU.add))
            link(nc.vector.reciprocal(stats[:, 1, :], stats[:, 0, :]))
            link(nc.vector.tensor_tensor(level[:], squares[:], along(stats[:, 1, :], EXPERTS), ALU.mult))
            link(nc.vector.tensor_copy(halves[:, :, 0, :].bitcast(F32R), level[:]))
            nc.vector.tensor_tensor(halves[:, :, 1, :], level[:], halves[:, :, 0, :],
                                    ALU.subtract).then_inc(halves_done, 1)

        @block.vector
        def _(dve):
            link = linked(dve)
            nc.vector.memset(gate_w[:], 0.0).then_inc(zeroed, 1)
            nc.vector.memset(logits[:, :, EXPERTS:], GUARD)
            for tiles in PARTS:
                centre(nc, link, h2[:, tiles], centred[:, tiles], squares[:, tiles],
                       stats[:, :, tiles]).then_inc(variance_done, 1)
            for n, tiles in enumerate(PARTS):
                dve.wait_ge(root_done, n + 1)
                invert_root(nc, link, stats[:, :, tiles])
                nc.vector.tensor_tensor(y2[:, tiles, 0, :], centred[:, tiles],
                                        along(stats[:, 2, tiles], D), ALU.mult).then_inc(norm_done, 1)
            mover_program("dve", dve)
            for e in moved:
                dve.wait_ge(moved[e], ROUTING.moved[e])
            with dve.Fori(0, 4) as g:
                for n in range(EB):
                    dve.wait_ge(spread, g * EB + (n + 1))
                    nc.vector.tensor_tensor(weighted[:, n % PB, :], slots[:, n % PB, :],
                                            y_t[:, bass.ds(g * SLOT, SLOT)], ALU.mult).then_inc(weigh, 1)
            dve.wait_ge(weights_in, 96)
            nc.vector.tensor_tensor(level[:], y2[:, :, 0, :], across(vectors[:, 0, :], TILES),
                                    ALU.add).then_inc(chain, 1)
            steps[0] += 1
            dve.wait_ge(chain, steps[0])
            for i, tiles in enumerate(PARTS):
                dve.wait_ge(projected, i + 1)
                part = level[:, tiles].rearrange("p (a h t) d -> p a h (t d)", a=2, h=2)
                link(nc.vector.tensor_tensor(
                    part, slots[:, i, :].rearrange("p (h a n) -> p a h n", a=2, h=2), part, ALU.add))
                centre(nc, link, level[:, tiles], centred[:, tiles], squares[:, tiles],
                       stats[:, :, tiles]).then_inc(variance_done, 1)
            for n, tiles in enumerate(PARTS):
                dve.wait_ge(root_done, 2 + n + 1)
                invert_root(nc, link, stats[:, :, tiles])
                part = level[:, tiles]
                link(nc.vector.tensor_tensor(part, centred[:, tiles], along(stats[:, 2, tiles], D), ALU.mult))
                link(nc.vector.tensor_tensor(part, part, across(vectors[:, 1, :], TILES // 2), ALU.mult))
                link(nc.vector.tensor_tensor(centred[:, tiles], h2[:, tiles],
                                             across(vectors[:, 2, :], TILES // 2), ALU.add))
                nc.vector.tensor_tensor(squares[:, tiles], part, centred[:, tiles],
                                        ALU.add).then_inc(result, 1)

        @block.scalar
        def _(act):
            for n, tiles in enumerate(PARTS):
                act.wait_ge(variance_done, n + 1)
                root(nc, stats[:, :, tiles]).then_inc(root_done, 1)
            for n, tiles in enumerate(PARTS):
                act.wait_ge(norm_done, n + 1)
                nc.scalar.copy(y2[:, tiles, 1, :], y2[:, tiles, 0, :]).then_inc(copied, 1)
            mover_program("act", act)
            act.sem_inc(mixed_out, 1)
            with act.Fori(0, 4) as g:
                act.wait_ge(summed, g + 1)
                nc.scalar.copy(mixed[:, bass.ds(g, 1), :].rearrange("p a n -> p (a n)"),
                               slots[:, SLOTS - 1, 0:512]).then_inc(mixed_out, 1)
            for n, tiles in enumerate(PARTS):
                act.wait_ge(variance_done, 2 + n + 1)
                root(nc, stats[:, :, tiles]).then_inc(root_done, 1)


def build(nc, x, x_turned, fc0, fc0_t, sw, cwt, cb, fc1_w, fc1_b, fc2_w, fc2_b, wqkv, gate_t, lattice,
          out_wt, out_b, ln_g, ln_b, k_fwd_rows, k_fwd_cols, k_inv_rows, k_inv_cols, k_lift_mask,
          k_rope, k_decay, k_select,
          k_ident, out):
    h_dram = nc.dram_tensor("h_scratch", (HH, IMAGES // QB, QB * WW), F32, kind="Internal").ap()
    with (
        nc.psum_tensor("slots", [128, SLOTS, SLOT], F32) as slots,
        nc.sbuf_tensor("ident", [128, 128], F32) as ident,
        nc.semaphore("ident_in") as ident_in,
    ):
        nc.sync.dma_start(ident[:, :], k_ident).then_inc(ident_in, 16)
        tower(nc, slots, ident, ident_in, h_dram, x, x_turned, fc0, fc0_t, sw, cwt, cb, fc1_w, fc1_b, fc2_w,
              fc2_b, k_fwd_rows, k_fwd_cols, k_inv_rows, k_inv_cols, k_lift_mask)
        with nc.sbuf_tensor("h2", [128, TILES, D], F32) as h2:
            attention(nc, slots, ident, h2, h_dram, wqkv, k_rope, k_decay)
            experts(nc, slots, ident, h2, gate_t, lattice, out_wt, out_b, ln_g, ln_b, k_select, out)


def kernel(**inputs):
    import numpy as _np
    import concourse.bacc as _bacc
    from concourse import mybir as _mybir
    from concourse.bass_utils import run_bass_kernel_spmd as _run

    f = {n: _np.asarray(a) for n, a in inputs.items()}
    t = "L0_tok_"
    order = [(n + 1) % LAYERS for n in range(LAYERS)]
    sw = [f[f"{t}sw{n}"].transpose(3, 0, 2, 1) for n in order[1:] + order[:1]]
    sw = _np.stack(sw).reshape(LAYERS, BLOCKS, 4, CH, MODES, CH).transpose(0, 2, 3, 1, 4, 5)
    x = _np.concatenate([f["x"], _np.ones((IMAGES, HH, WW, 1), _np.float32)], axis=3)
    fc0 = _np.concatenate([f[t + "fc0_w"], f[t + "fc0_b"][None, :]], axis=0)
    wq, wk = f["L0_attn_W_Q"], f["L0_attn_W_K"]
    fwd_rows, fwd_cols, inv_rows, inv_cols = dft_constants()
    rope, decay, select = attention_constants()
    arrays = {
        "x": x.reshape(GROUPS, GB, 2, 4, 8, WW, IN_CH).transpose(0, 1, 3, 6, 4, 2, 5).reshape(
            GROUPS, GB * 4 * IN_CH, PART),
        "x_turned": _np.roll(x, -GB, axis=0).reshape(GROUPS, QUADS, 2, 2, 2, 4, 8, WW, IN_CH).transpose(
            0, 5, 2, 6, 4, 1, 8, 3, 7).reshape(GROUPS, 128, QUADS * IN_CH * 2 * WW),
        "fc0": _np.tile(fc0, (128 // IN_CH, 1)), "fc0_t": fc0.T,
        "sw": sw.reshape(LAYERS, 128, BLOCKS * MODES * CH),
        "cwt": _np.stack([f[f"{t}cw{n}"].T for n in order]),
        "cb": _np.stack([f[f"{t}cb{n}"] for n in order], axis=1),
        "fc1_w": f[t + "fc1_w"], "fc1_b": f[t + "fc1_b"],
        "fc2_w": f[t + "fc2_w"], "fc2_b": f[t + "fc2_b"],
        "wqkv": _np.concatenate([wq, wk, f["L0_attn_W_V"]], axis=1),
        "gate_t": f["L0_ffn_gate_w"].T,
        "lattice": f["L0_ffn_lattice_weights"].reshape(EXPERTS // 2, 2, D, D).transpose(
            1, 2, 0, 3).reshape(128, -1),
        "out_wt": f["L0_ffn_out_w"].T, "out_b": f["L0_ffn_out_b"],
        "ln_g": f["L0_ffn_ln_g"], "ln_b": f["L0_ffn_ln_b"],
        "k_fwd_rows": fwd_rows, "k_fwd_cols": fwd_cols,
        "k_inv_rows": inv_rows, "k_inv_cols": inv_cols, "k_lift_mask": lift_mask(),
        "k_rope": rope, "k_decay": decay, "k_select": select,
        "k_ident": _np.eye(128, dtype=_np.float32),
    }
    nc = _bacc.Bacc("TRN2", target_bir_lowering=False, num_devices=1)
    arrays = {f"in_{n}_dram": _np.ascontiguousarray(a) for n, a in arrays.items()}
    args = [nc.dram_tensor(n, a.shape, _mybir.dt.from_np(a.dtype), kind="ExternalInput").ap()
            for n, a in arrays.items()]
    out = nc.dram_tensor("out_0_dram", (IMAGES, HH, WW), _mybir.dt.float32, kind="ExternalOutput").ap()
    build(nc, *args, out)
    r = _run(nc, [arrays], core_ids=[0])
    return r.results[0]["out_0_dram"]
```
